# Optimizing a Trainium2 kernel written in Bass

```python
import numpy as np
import jax
import jax.numpy as jnp

def _softmax(x, axis=-1):
    return jax.nn.softmax(x, axis=axis)

def _gelu(x):
    return jax.nn.gelu(x, approximate=True)

def _silu(x):
    return jax.nn.silu(x)

def _sigmoid(x):
    return jax.nn.sigmoid(x)

def _layernorm(x, axis=-1, eps=1e-05):
    m = jnp.mean(x, axis=axis, keepdims=True)
    v = jnp.var(x, axis=axis, keepdims=True)
    return (x - m) / jnp.sqrt(v + eps)

def _scatter_add(tgt, idx, src, axis=0):
    return tgt.at[idx].add(src)

def _segment_sum(src, seg, n):
    return jax.ops.segment_sum(src, seg, n)
kernel_name = 'mk_decoder_preln_d1_seqx_r4_b31d0b'

def setup_inputs(seed: int=0):
    np.random.seed(seed)
    _w = jnp.asarray

    def _rec_inputs():
        import jax
        import jax.numpy as jnp
        _rk = jax.random.key(seed)
        x = 0.0002417 + 0.9998 * jax.random.normal(jax.random.fold_in(_rk, 1), (32, 112, 256), jnp.float32)
        _lenS = 112 - jax.random.randint(jax.random.fold_in(_rk, 7), (32,), 0, max(1, 112 // 4) + 1, jnp.int32)
        _lenS2 = 375 - jax.random.randint(jax.random.fold_in(_rk, 8), (32,), 0, max(1, 375 // 4) + 1, jnp.int32)
        _ctx_1024P = jax.random.normal(jax.random.fold_in(_rk, 11), (32, 16, 256), jnp.float32)
        _ctx_1024c = jax.random.dirichlet(jax.random.fold_in(_rk, 511), 0.3 * jnp.ones((16,), jnp.float32), (32, 375))
        _ctx_1024t = jnp.einsum('bsk,bkd->bsd', _ctx_1024c, _ctx_1024P)
        _ctx_1024t = _ctx_1024t * jax.lax.rsqrt(jnp.mean(jnp.square(_ctx_1024t)) + 1e-12) * 0.953939
        ctx_1024 = 7.22013e-05 + 1.00017 * (_ctx_1024t + 0.3 * jax.random.normal(jax.random.fold_in(_rk, 611), (32, 375, 256), jnp.float32))
        return (x, ctx_1024)
    x, ctx_1024 = _rec_inputs()

    def _L0_attn_setup():
        import jax, jax.numpy as jnp
        import numpy as np
        D_MODEL = 256
        N_HEADS = 16
        HEAD_D = D_MODEL // N_HEADS
        B, T = (4, 1024)
        ROPE_BASE = 10000.0

        def _rope(x):
            Bx, Tx, Dx = x.shape
            half = Dx // 2
            inv_freq = 1.0 / ROPE_BASE ** (jnp.arange(half, dtype=jnp.float32) / half)
            ang = jnp.arange(Tx, dtype=jnp.float32)[:, None] * inv_freq[None, :]
            cos, sin = (jnp.cos(ang), jnp.sin(ang))
            x1 = x[..., 0::2]
            x2 = x[..., 1::2]
            r1 = x1 * cos - x2 * sin
            r2 = x1 * sin + x2 * cos
            out = jnp.stack([r1, r2], axis=-1).reshape(Bx, Tx, Dx)
            return out
        key = jax.random.key(seed)
        k_x, k_q, k_k, k_v = jax.random.split(key, 4)
        x = jax.random.normal(k_x, (B, T, D_MODEL), dtype=jnp.float32)
        bound = np.sqrt(6.0 / (HEAD_D * N_HEADS))
        shp = (HEAD_D, HEAD_D, N_HEADS)
        w_q = jax.random.uniform(k_q, shp, jnp.float32, -bound, bound)
        w_k = jax.random.uniform(k_k, shp, jnp.float32, -bound, bound)
        w_v = jax.random.uniform(k_v, shp, jnp.float32, -bound, bound)
        return {'x': x, 'w_q': w_q, 'w_k': w_k, 'w_v': w_v}
    _L0_attn_all = _L0_attn_setup()
    _L0_attn_in = {k: v for k, v in _L0_attn_all.items() if k in ('w_q', 'w_k', 'w_v')}
    del _L0_attn_all

    def _L0_xattn_setup():
        import jax, jax.numpy as jnp
        import numpy as np
        D_MODEL = 256
        B, S = (4, 512)
        key = jax.random.key(seed)
        ks = jax.random.split(key, 10)
        s = 1.0 / np.sqrt(D_MODEL)
        return {'k': jax.random.normal(ks[0], (B, S, D_MODEL), jnp.float32), 'v': jax.random.normal(ks[1], (B, S, D_MODEL), jnp.float32), 'q': jax.random.normal(ks[2], (B, S, D_MODEL), jnp.float32), 'Wk': jax.random.normal(ks[3], (D_MODEL, D_MODEL), jnp.float32) * s, 'Wv': jax.random.normal(ks[4], (D_MODEL, D_MODEL), jnp.float32) * s, 'bv': jnp.zeros((D_MODEL,), jnp.float32), 'Wq': jax.random.normal(ks[5], (D_MODEL, D_MODEL), jnp.float32) * s, 'bq': jnp.zeros((D_MODEL,), jnp.float32), 'Wo': jax.random.normal(ks[6], (D_MODEL, D_MODEL), jnp.float32) * s, 'bo': jnp.zeros((D_MODEL,), jnp.float32)}
    _L0_xattn_all = _L0_xattn_setup()
    _L0_xattn_in = {k: v for k, v in _L0_xattn_all.items() if k in ('Wk', 'Wv', 'bv', 'Wq', 'bq', 'Wo', 'bo')}
    del _L0_xattn_all

    def _L0_ffn_setup():
        import jax, jax.numpy as jnp
        import numpy as np
        EMBED_DIM = 256
        NUM_EXPERTS = 8
        B, S = (2, 512)
        key = jax.random.key(seed)
        ks = jax.random.split(key, 5)
        scale = 1.0 / np.sqrt(EMBED_DIM)
        x = jax.random.normal(ks[0], (B, S, EMBED_DIM), dtype=jnp.float32)
        router_w = jax.random.normal(ks[1], (NUM_EXPERTS, EMBED_DIM), dtype=jnp.float32) * scale
        router_b = jnp.zeros((NUM_EXPERTS,), dtype=jnp.float32)
        expert_w = jax.random.normal(ks[2], (NUM_EXPERTS, EMBED_DIM, EMBED_DIM), dtype=jnp.float32) * scale
        expert_b = jnp.zeros((NUM_EXPERTS, EMBED_DIM), dtype=jnp.float32)
        return {'x': x, 'router_w': router_w, 'router_b': router_b, 'expert_w': expert_w, 'expert_b': expert_b}
    _L0_ffn_all = _L0_ffn_setup()
    _L0_ffn_in = {k: v for k, v in _L0_ffn_all.items() if k in ('router_w', 'router_b', 'expert_w', 'expert_b')}
    del _L0_ffn_all
    return {'x': x, 'ctx_1024': ctx_1024, 'L0_attn_w_q': _L0_attn_in['w_q'], 'L0_attn_w_k': _L0_attn_in['w_k'], 'L0_attn_w_v': _L0_attn_in['w_v'], 'L0_xattn_Wk': _L0_xattn_in['Wk'], 'L0_xattn_Wv': _L0_xattn_in['Wv'], 'L0_xattn_bv': _L0_xattn_in['bv'], 'L0_xattn_Wq': _L0_xattn_in['Wq'], 'L0_xattn_bq': _L0_xattn_in['bq'], 'L0_xattn_Wo': _L0_xattn_in['Wo'], 'L0_xattn_bo': _L0_xattn_in['bo'], 'L0_ffn_router_w': _L0_ffn_in['router_w'], 'L0_ffn_router_b': _L0_ffn_in['router_b'], 'L0_ffn_expert_w': _L0_ffn_in['expert_w'], 'L0_ffn_expert_b': _L0_ffn_in['expert_b']}

def reference(x, ctx_1024, L0_attn_w_q, L0_attn_w_k, L0_attn_w_v, L0_xattn_Wk, L0_xattn_Wv, L0_xattn_bv, L0_xattn_Wq, L0_xattn_bq, L0_xattn_Wo, L0_xattn_bo, L0_ffn_router_w, L0_ffn_router_b, L0_ffn_expert_w, L0_ffn_expert_b):
    import jax
    import jax.numpy as jnp

    def _L0_attn_ref(x, w_q, w_k, w_v):
        import jax, jax.numpy as jnp
        import numpy as np
        D_MODEL = 256
        N_HEADS = 16
        HEAD_D = D_MODEL // N_HEADS
        B, T = (4, 1024)
        ROPE_BASE = 10000.0

        def _rope(x):
            Bx, Tx, Dx = x.shape
            half = Dx // 2
            inv_freq = 1.0 / ROPE_BASE ** (jnp.arange(half, dtype=jnp.float32) / half)
            ang = jnp.arange(Tx, dtype=jnp.float32)[:, None] * inv_freq[None, :]
            cos, sin = (jnp.cos(ang), jnp.sin(ang))
            x1 = x[..., 0::2]
            x2 = x[..., 1::2]
            r1 = x1 * cos - x2 * sin
            r2 = x1 * sin + x2 * cos
            out = jnp.stack([r1, r2], axis=-1).reshape(Bx, Tx, Dx)
            return out
        Bx, Tx, Dx = x.shape
        d = Dx // N_HEADS
        xh = x.reshape(Bx, Tx, d, N_HEADS)
        q = jnp.einsum('btqh,qdh->btdh', xh, w_q).reshape(Bx, Tx, Dx)
        k = jnp.einsum('btkh,kdh->btdh', xh, w_k).reshape(Bx, Tx, Dx)
        v = jnp.einsum('btvh,vdh->btdh', xh, w_v).reshape(Bx, Tx, Dx)
        q = _rope(q)
        k = _rope(k)
        gamma = 1.0 / jnp.sqrt(jnp.float32(Dx))
        scores = jnp.einsum('bqd,bkd->bqk', q, k) * gamma
        causal = jnp.tril(jnp.ones((Tx, Tx), dtype=bool))
        scores = jnp.where(causal[None], scores, -jnp.inf)
        attn = jax.nn.softmax(scores, axis=-1)
        y = jnp.einsum('bqt,btd->bqd', attn, v)
        return y

    def _L0_xattn_ref(k, v, q, Wk, Wv, bv, Wq, bq, Wo, bo):
        import jax, jax.numpy as jnp
        import numpy as np
        D_MODEL = 256
        B, S = (4, 512)
        kp = jnp.einsum('bsd,ed->bse', k, Wk)
        vp = jnp.einsum('bsd,ed->bse', v, Wv) + bv
        qp = jnp.einsum('bsd,ed->bse', q, Wq) + bq
        scale = 1.0 / jnp.sqrt(jnp.float32(kp.shape[-1]))
        scores = jnp.einsum('bqd,bkd->bqk', qp, kp) * scale
        probs = jax.nn.softmax(scores, axis=-1)
        ctx = jnp.einsum('bqk,bkd->bqd', probs, vp)
        return jnp.einsum('bqd,ed->bqe', ctx, Wo) + bo

    def _L0_ffn_ref(x, router_w, router_b, expert_w, expert_b):
        import jax, jax.numpy as jnp
        import numpy as np
        EMBED_DIM = 256
        NUM_EXPERTS = 8
        B, S = (2, 512)
        Bb, Ss, D = x.shape
        xt = x.reshape(-1, D)
        logits = xt @ router_w.T + router_b
        probs = jax.nn.softmax(logits, axis=-1)
        idx = jnp.argmax(logits, axis=-1)
        w = jnp.take_along_axis(probs, idx[:, None], axis=1)[:, 0]
        y_all = jnp.einsum('td,efd->tef', xt, expert_w) + expert_b
        y = jnp.take_along_axis(y_all, idx[:, None, None], axis=1)[:, 0]
        out = (y * w[:, None]).reshape(Bb, Ss, D)
        return out
    x = x + _L0_attn_ref(_layernorm(x, axis=-1), L0_attn_w_q, L0_attn_w_k, L0_attn_w_v)
    x = x + _L0_xattn_ref(ctx_1024, ctx_1024, _layernorm(x, axis=-1), L0_xattn_Wk, L0_xattn_Wv, L0_xattn_bv, L0_xattn_Wq, L0_xattn_bq, L0_xattn_Wo, L0_xattn_bo)
    x = x + _L0_ffn_ref(_layernorm(x, axis=-1), L0_ffn_router_w, L0_ffn_router_b, L0_ffn_expert_w, L0_ffn_expert_b)
    return x

_drawn_inputs = setup_inputs


def setup_inputs(seed=0):
    import zlib

    import numpy as np

    out = dict(_drawn_inputs(seed))
    spreads = {'L0_xattn_bv': (0.0, 0.1),
     'L0_xattn_bq': (0.0, 0.1),
     'L0_xattn_bo': (0.0, 0.1),
     'L0_ffn_router_b': (0.0, 0.1),
     'L0_ffn_expert_b': (0.0, 0.1)}
    factors = {'L0_attn_w_q': 3.042, 'L0_attn_w_k': 3.393}
    for name, (base, spread) in spreads.items():
        noise = np.random.default_rng([zlib.crc32(name.encode()), seed]).standard_normal(out[name].shape)
        drawn = base * np.exp(spread * noise) if base else spread * noise
        out[name] = jnp.asarray(drawn.astype(out[name].dtype))
    for name, factor in factors.items():
        out[name] = (out[name] * factor).astype(out[name].dtype)
    return out
```

```python
from contextlib import ExitStack

import numpy as np

import concourse.bass as bass
from concourse import mybir

F32 = mybir.dt.float32
BF16 = mybir.dt.bfloat16
I32 = mybir.dt.int32
U32 = mybir.dt.uint32
ALU = mybir.AluOpType
ACT = mybir.ActivationFunctionType
AX = mybir.AxisListType

B, T, D = 32, 112, 256
S = 375
H = 16
E = 8
P = 128
G = 2
NP = B // G
GT = G * T
HALF = D // P
ST = -(-S // P)
NAT = ST * D
TRN = HALF * S
CW = NAT + TRN
SCALE = float(D) ** -0.5
EPS = 1e-5
NEG = -1e30

C_RSTD, C_SHIFT, C_PROB, C_ID, ROW = D, D + 1, D + 2, D + 3, D + 4
NTOK = B * T
CAP = NTOK + P
TILES = NTOK // P + E - 1
IDLE = E - 1
SCR = E * CAP + IDLE * P
NO_TOKEN = 1 << 20
RING = 5

K_ID, K_COS, K_SIN, K_MASK, K_UP, K_IOTA, K_EXP, K_TILE = np.cumsum(
    [0, P, HALF * GT, HALF * GT, T, T, G * E, E]).tolist()
K_END = K_TILE + TILES + 1


def wait(eng, sem, n):
    if isinstance(n, int) and n <= 0:
        return
    eng.wait_ge(sem, n)


def build(nc, x, ctxs, consts, w_self, w_fold, b_fold, w_router, w_expert, b_expert, out):
    with ExitStack() as stack:
        def sb(name, shape, dt=F32):
            return stack.enter_context(nc.sbuf_tensor(name, shape, dt))

        def sem(name):
            return stack.enter_context(nc.semaphore(name))

        scratch = nc.dram_tensor("routed_rows", (SCR, ROW), F32).ap()
        x_rows = x.rearrange("b t d -> (b t) d")
        out_rows = out.rearrange("b t d -> (b t) d")

        cst = sb("cst", [P, K_END])
        ident = cst[:, K_ID:K_ID + P]
        cos2 = cst[:, K_COS:K_COS + HALF * GT]
        sin2 = cst[:, K_SIN:K_SIN + HALF * GT]
        causal = cst[0:T, K_MASK:K_MASK + T]
        iota = cst[0:T, K_IOTA:K_IOTA + G * E].rearrange("t (g e) -> t g e", g=G)
        up = sb("up", [T, T], BF16)
        ones = sb("ones", [T, T], BF16)
        wself = sb("wself", [P, 3, HALF, P])
        wfold = sb("wfold", [P, 4, HALF, D])
        bfold = sb("bfold", [P, HALF + HALF * T + D])
        wqk = sb("wqk", [P, HALF, D])
        wvo = sb("wvo", [P, HALF, D])
        bqk = sb("bqk", [P, HALF])
        bvo = sb("bvo", [T, D])
        wrt = sb("wrt", [P, HALF * E + G * E])
        wexp = sb("wexp", [P, E * HALF * D])
        bexp = sb("bexp", [P, E * D])
        padt = sb("padt", [P, ROW])
        mhalf = sb("mhalf", [P, G])
        step_ids = sb("step_ids", [T, G], I32)

        xs = sb("xs", [T, 2, G, D])
        h1 = sb("h1", [T, G, D])
        h1T = sb("h1T", [P, HALF, G, T])
        tq = sb("tq", [P, 2, HALF, GT])
        tk = sb("tk", [P, 2, HALF, GT])
        qr = sb("qr", [P, HALF, G, T])
        kr = sb("kr", [P, HALF, G, T])
        v = sb("v", [T, G, D])
        sm = sb("sm", [T, G, T])
        p1 = sb("p1", [T, G, T])
        p1T = sb("p1T", [T, G, T])
        mx1 = sb("mx1", [T, G])
        nb1 = sb("nb1", [T, G])
        sum1 = sb("sum1", [T, G])
        ri1 = sb("ri1", [T, G])
        cx = sb("cx", [P, 2, G, CW])
        x1 = sb("x1", [T, 2, G, D])
        x1b = sb("x1b", [T, 2, G, D])
        h2 = sb("h2", [T, G, D])
        h2T = sb("h2T", [P, HALF, G, T])
        qt = sb("qt", [P, HALF, G, T])
        xp = sb("xp", [T, G, ST * P])
        xpT = sb("xpT", [P, G, ST, T])
        zT = sb("zT", [P, HALF, G, T])
        mxx = sb("mxx", [T, G])
        nbx = sb("nbx", [T, G])
        sumx = sb("sumx", [T, G])
        rix = sb("rix", [T, G])
        row = sb("row", [T, 2, G, ROW])
        row_int = row[:, :, :, :].bitcast(I32)
        h3 = sb("h3", [T, G, D])
        h3T = sb("h3T", [P, HALF, G, T])
        lg = sb("lg", [T, G, E])
        mxr = sb("mxr", [T, G, 1])
        dif = sb("dif", [T, G, E])
        er = sb("er", [T, G, E])
        sr = sb("sr", [T, G])
        key = sb("key", [T, G, E])
        key2 = sb("key2", [T, G, E])
        idx = sb("idx", [T, G, 1])
        oh = sb("oh", [T, G, E], BF16)
        rk = sb("rk", [T, G, E])
        rk2 = sb("rk2", [T, G, E])
        base = sb("base", [T, 2, E])
        posf = sb("posf", [T, G])
        pos = sb("pos", [T, 2, G], I32)
        st = [sb(f"st{n}", [T, G, 6]) for n in range(3)]
        mv = [sb(f"mv{n}", [T, G, 2]) for n in range(3)]
        ve = [sb(f"ve{n}", [T, G]) for n in range(3)]
        nmean = [sb(f"nmean{n}", [T, G]) for n in range(3)]
        rs = [sb(f"rs{n}", [T, G]) for n in range(3)]
        nm = [sb(f"nm{n}", [T, G]) for n in range(3)]
        cnt = sb("cnt", [1, E])
        big = sb("big", [1, E, NTOK // P])
        til = sb("til", [1, E])
        cum = sb("cum", [1, E])
        ge = sb("ge", [1, TILES, E])
        gt = sb("gt", [1, TILES, E])
        ex = sb("ex", [1, TILES])
        beg = sb("beg", [1, TILES])
        off1 = sb("off1", [1, TILES])
        off2 = sb("off2", [1, TILES])
        exc = sb("exc", [1, TILES])
        tab_row = sb("tab_row", [1, TILES], I32)
        tab_w = sb("tab_w", [1, TILES], I32)
        tab_b = sb("tab_b", [1, TILES], I32)
        tab_pad = sb("tab_pad", [1, E], I32)
        er_rows = sb("er_rows", [P, RING, ROW])
        er_ids = er_rows[:, :, :].bitcast(U32)
        eh = sb("eh", [P, RING, D])
        ehT = sb("ehT", [P, RING, HALF, P])
        ey = sb("ey", [P, RING, D])
        eo = sb("eo", [P, RING, D])

        bank = [stack.enter_context(nc.psum_tensor(f"bank{n}", [P, 512], F32)) for n in range(8)]
        ps_T = bank[0][:, 0:HALF * GT].rearrange("p (c g t) -> p c g t", c=HALF, g=G)
        ps_q = bank[1][:, 0:HALF * GT].rearrange("p (c n) -> p c n", c=HALF)
        ps_k = bank[2][:, 0:HALF * GT].rearrange("p (c n) -> p c n", c=HALF)
        ps_v = bank[3][0:T, :].rearrange("t (g d) -> t g d", g=G)
        ps_y = ps_v
        ps_s = bank[4][0:T, 0:GT].rearrange("t (g k) -> t g k", g=G)
        ps_pT = bank[4][0:T, GT:2 * GT].rearrange("t (g k) -> t g k", g=G)
        ps_lg = bank[4][0:T, 2 * GT:2 * GT + G * E].rearrange("t (g e) -> t g e", g=G)
        ps_rk = bank[4][0:T, 2 * GT + G * E:2 * GT + 2 * G * E].rearrange("t (g e) -> t g e", g=G)
        ps_tot = bank[4][0:T, 2 * GT + 2 * G * E:2 * GT + 2 * G * E + E]
        ps_qt = bank[5][:, 0:HALF * GT].rearrange("p (c g t) -> p c g t", c=HALF, g=G)
        ps_z = ps_qt
        ps_xs = [bank[6 + g][0:T, 0:S] for g in range(G)]
        ps_xpT = [bank[6 + g][:, 0:ST * T].rearrange("p (n t) -> p n t", n=ST) for g in range(G)]
        ps_o = bank[6][0:T, :].rearrange("t (g d) -> t g d", g=G)

        l_cst, l_self, l_fold, l_bfold, l_router, l_wexp, l_bexp = (
            sem(n) for n in ("l_cst", "l_self", "l_fold", "l_bfold", "l_router", "l_wexp", "l_bexp"))
        l_x = [sem(f"l_x{n}") for n in range(2)]
        l_cx = [sem(f"l_cx{n}") for n in range(2)]
        s_scat = [sem(f"s_scat{n}") for n in range(2)]
        s_idle, s_pad = sem("s_idle"), sem("s_pad")
        l_rows = [sem(f"l_rows{n}") for n in range(RING)]
        s_out = [sem(f"s_out{n}") for n in range(RING)]
        (pe_h1T, pe_q, pe_k, pe_v, pe_s, pe_pT, pe_y, pe_h2T, pe_qt, pe_xs, pe_xpT, pe_z, pe_o, pe_h3T,
         pe_lg, pe_rank, pe_fold, pe_eT, pe_ey) = (sem(n) for n in (
            "pe_h1T pe_q pe_k pe_v pe_s pe_pT pe_y pe_h2T pe_qt pe_xs pe_xpT pe_z pe_o pe_h3T "
            "pe_lg pe_rank pe_fold pe_eT pe_ey").split())
        (a_h1, a_h1T, a_v, a_p1, a_pT, a_h2, a_h2T, a_qt, a_xp, a_xpT, a_z, a_h3, a_h3T, a_er, a_fold,
         a_eh, a_ehT) = (sem(n) for n in (
            "a_h1 a_h1T a_v a_p1 a_pT a_h2 a_h2T a_qt a_xp a_xpT a_z a_h3 a_h3T a_er a_fold "
            "a_eh a_ehT").split())
        (d_const, d_tq, d_tk, d_max1, d_nb1, d_ri1, d_x1, d_maxx, d_nbx, d_rix, d_x2, d_lg, d_mxr, d_dif, d_sr, d_w,
         d_key, d_key2, d_idx, d_oh, d_rk2, d_posf, d_pos, d_base, d_bvo, d_tab, d_ey, d_eo) = (sem(n) for n in (
            "d_const d_tq d_tk d_max1 d_nb1 d_ri1 d_x1 d_maxx d_nbx d_rix d_x2 d_lg d_mxr d_dif d_sr d_w "
            "d_key d_key2 d_idx d_oh d_rk2 d_posf d_pos d_base d_bvo d_tab d_ey d_eo").split())
        d_st = [sem(f"d_st{n}") for n in range(3)]
        d_mv = [sem(f"d_mv{n}") for n in range(3)]
        d_ve = [sem(f"d_ve{n}") for n in range(3)]
        g_const, g_q, g_k, g_x1b, g_id = (sem(n) for n in "g_const g_q g_k g_x1b g_id".split())
        d_gate, g_gate = sem("d_gate"), sem("g_gate")
        g_pow = [sem(f"g_pow{n}") for n in range(3)]
        g_rs = [sem(f"g_rs{n}") for n in range(3)]

        def live(p):
            return not isinstance(p, int) or 0 <= p < NP

        def steps(eng, step):
            for s in range(-1, 2):
                step(s, s % 2)
            with eng.Fori(1, NP // 2 - 1) as i:
                for k in range(2):
                    step(i * 2 + k, k)
            for s in range(NP - 2, NP + 1):
                step(s, s % 2)

        block = stack.enter_context(nc.Block())

        @block.sync
        def _(sp):
            def load_x(p, slot):
                wait(sp, d_x1, p - 1)
                sp.dma_start(xs[:, slot], x_rows[bass.ds(p * GT, GT), :].rearrange("(g t) d -> t g d", g=G)
                             ).then_inc(l_x[slot], 16)

            def load_ctx(p, slot):
                wait(sp, pe_z, p - 1)
                sp.dma_start(cx[:, slot].rearrange("p g c -> p (g c)"), ctxs[bass.ds(p * P, P), :]
                             ).then_inc(l_cx[slot], 16)

            load_x(0, 0)
            sp.dma_start(cst[:, :], consts).then_inc(l_cst, 16)
            load_ctx(0, 0)
            sp.dma_start(wrt[:, :], w_router).then_inc(l_router, 16)

            def step(s, k):
                if live(s + 2):
                    load_x(s + 2, k)
                    load_ctx(s + 2, k)
                if isinstance(s, int) and s == 0:
                    sp.dma_start(wexp[:, :], w_expert).then_inc(l_wexp, 16)
                    sp.dma_start(bexp[:, :], b_expert).then_inc(l_bexp, 16)
                    wait(sp, g_const, 2)
                    sp.dma_start(scratch[E * CAP:SCR, :].rearrange("(n p) c -> p n c", p=P),
                                 padt[:, :].rearrange("p (a c) -> p a c", a=1).to_broadcast([P, IDLE, ROW])
                                 ).then_inc(s_idle, 16)

            steps(sp, step)

            sp.wait_ge(d_tab, 4)
            for n in range(2):
                sp.wait_ge(s_scat[n], 16 * G * NP // 2)
            for e in range(E):
                r = sp.value_load(tab_pad[0:1, e:e + 1], min_val=e * CAP, max_val=e * CAP + NTOK)
                sp.dma_start(scratch[bass.ds(r, P), :], padt[:, :]).then_inc(s_pad, 16)
            sp.wait_ge(s_idle, 16)
            sp.wait_ge(s_pad, 16 * E)

            def tile(j, k, turn):
                wait(sp, s_out[k], turn * 16)
                r = sp.value_load(tab_row[0:1, bass.ds(j, 1)], min_val=0, max_val=SCR - P)
                sp.dma_start(er_rows[:, k, :], scratch[bass.ds(r, P), :]).then_inc(l_rows[k], 16)

            for k in range(RING):
                tile(k, k, 0)
            with sp.Fori(1, TILES // RING) as i:
                for k in range(RING):
                    tile(i * RING + k, k, i)
            for k in range(RING):
                sp.wait_ge(s_out[k], 16 * (TILES // RING))

        @block.tensor
        def _(pe):
            def first_transposes(p):
                wait(pe, a_h1, p + 1)
                wait(pe, a_h3T, p - 2)
                for c in range(HALF):
                    for g in range(G):
                        m = pe.transpose(ps_T[:, c, g], h1[:, g, c::2], ident[0:T, 0:T])
                m.then_inc(pe_h1T, 1)

            def first_qk(p):
                wait(pe, a_h1T, p + 1)
                for n, (ps, ready, used) in enumerate(((ps_q, pe_q, d_tq), (ps_k, pe_k, d_tk))):
                    wait(pe, used, p)
                    for c in range(HALF):
                        m = pe.matmul(ps[:, c], wself[:, n, c], h1T[:, c].rearrange("p g t -> p (g t)"),
                                      start=True, stop=True)
                    m.then_inc(ready, 1)

            def first_v(p):
                wait(pe, d_x1, p)
                for g in range(G):
                    for c in range(HALF):
                        m = pe.matmul(ps_v[:, g, c * P:(c + 1) * P], h1T[:, c, g], wself[:, 2, c],
                                      start=True, stop=True)
                m.then_inc(pe_v, 1)

            def first_scores(p):
                wait(pe, g_q, p + 1)
                wait(pe, g_k, p + 1)
                wait(pe, d_max1, p * G)
                wait(pe, d_lg, p - 1)
                for g in range(G):
                    for c in range(HALF):
                        m = pe.matmul(ps_s[:, g], qr[:, c, g], kr[:, c, g], start=(c == 0), stop=(c == HALF - 1))
                m.then_inc(pe_s, 1)

            def first_probs_T(p):
                wait(pe, a_p1, (p + 1) * G)
                for g in range(G):
                    m = pe.transpose(ps_pT[:, g], p1[:, g], ident[0:T, 0:T])
                m.then_inc(pe_pT, 1)

            def first_y(p):
                wait(pe, a_v, p + 1)
                wait(pe, a_pT, p + 1)
                for g in range(G):
                    m = pe.matmul(ps_y[:, g], p1T[:, g], v[:, g], start=True, stop=True)
                m.then_inc(pe_y, 1)

            def cross_transposes(p):
                wait(pe, a_h2, p + 1)
                if live(p + 1):
                    wait(pe, a_h1T, p + 2)
                for c in range(HALF):
                    for g in range(G):
                        m = pe.transpose(ps_T[:, c, g], h2[:, g, c * P:(c + 1) * P], ident[0:T, 0:T])
                m.then_inc(pe_h2T, 1)

            def cross_queries(p):
                wait(pe, a_h2T, p + 1)
                wait(pe, a_z, p)
                for c in range(HALF):
                    for n in range(HALF):
                        m = pe.matmul(ps_qt[:, c].rearrange("p g t -> p (g t)"), wqk[:, n, c * P:(c + 1) * P],
                                      h2T[:, n].rearrange("p g t -> p (g t)"), start=(n == 0), stop=(n == HALF - 1))
                m.then_inc(pe_qt, 1)

            def cross_scores(p, slot, count):
                wait(pe, a_qt, p + 1)
                pe.wait_ge(l_cx[slot], count)
                wait(pe, d_x2, p)
                for g in range(G):
                    wait(pe, a_xpT, (p - 1) * G + g + 1)
                    for c in range(HALF):
                        m = pe.matmul(ps_xs[g], qt[:, c, g], cx[:, slot, g, NAT + c * S:NAT + (c + 1) * S],
                                      start=(c == 0), stop=(c == HALF - 1))
                    m.then_inc(pe_xs, 1)

            def cross_probs_T(p):
                for g in range(G):
                    wait(pe, a_xp, p * G + g + 1)
                    for n in range(ST):
                        m = pe.transpose(ps_xpT[g][:, n], xp[:, g, n * P:(n + 1) * P], ident[0:T, 0:T])
                    m.then_inc(pe_xpT, 1)

            def cross_z(p, slot, g):
                wait(pe, a_xpT, p * G + g + 1)
                for c in range(HALF):
                    for n in range(ST):
                        m = pe.matmul(ps_z[:, c, g], cx[:, slot, g, n * D + c * P:n * D + (c + 1) * P],
                                      xpT[:, g, n], start=(n == 0), stop=(n == ST - 1))
                if g == G - 1:
                    m.then_inc(pe_z, 1)

            def cross_out(p):
                wait(pe, a_z, p + 1)
                for g in range(G):
                    for c in range(HALF):
                        m = pe.matmul(ps_o[:, g], zT[:, c, g], wvo[:, c], start=(c == 0), stop=(c == HALF - 1))
                m.then_inc(pe_o, 1)

            def router_transposes(p):
                wait(pe, a_h3, p + 1)
                if live(p + 1):
                    wait(pe, a_h2T, p + 2)
                for c in range(HALF):
                    for g in range(G):
                        m = pe.transpose(ps_T[:, c, g], h3[:, g, c * P:(c + 1) * P], ident[0:T, 0:T])
                m.then_inc(pe_h3T, 1)

            def router_logits(p):
                wait(pe, a_h3T, p + 1)
                wait(pe, d_base, p)
                for g in range(G):
                    for c in range(HALF):
                        m = pe.matmul(ps_lg[:, g], h3T[:, c, g], wrt[:, c * E:(c + 1) * E],
                                      start=(c == 0), stop=(c == HALF - 1))
                m.then_inc(pe_lg, 1)

            def ranks(p):
                wait(pe, d_oh, p + 1)
                if live(p + 2):
                    wait(pe, a_pT, p + 3)
                pe.matmul(ps_rk[:, 0], up[:, :], oh[:, 0], start=True, stop=True)
                pe.matmul(ps_rk[:, 1], up[:, :], oh[:, 1], start=True, stop=False)
                pe.matmul(ps_rk[:, 1], ones[:, :], oh[:, 0], start=False, stop=True)
                pe.matmul(ps_tot, ones[:, :], oh[:, 0], start=True, stop=False)
                pe.matmul(ps_tot, ones[:, :], oh[:, 1], start=False, stop=True).then_inc(pe_rank, 1)

            def fold_weights():
                pe.wait_ge(l_fold, 16)
                pe.wait_ge(l_bfold, 16)
                for n, (a, b, ps) in enumerate(((0, 1, bank[6]), (2, 3, bank[7]))):
                    for c in range(HALF):
                        for e in range(HALF):
                            m = pe.matmul(ps[:, c * D:(c + 1) * D], wfold[:, a, e, c * P:(c + 1) * P],
                                          wfold[:, b, e, :], start=(e == 0), stop=(e == HALF - 1))
                    m.then_inc(pe_fold, 1)
                for c in range(HALF):
                    for e in range(HALF):
                        pe.matmul(bank[5][:, c:c + 1], wfold[:, 1, e, c * P:(c + 1) * P], bfold[:, e:e + 1],
                                  start=(e == 0), stop=(e == HALF - 1))
                for e in range(HALF):
                    m = pe.matmul(bank[5][0:T, D:2 * D], bfold[:, HALF + e * T:HALF + (e + 1) * T],
                                  wfold[:, 3, e, :], start=(e == 0), stop=(e == HALF - 1))
                m.then_inc(pe_fold, 1)

            pe.wait_ge(l_cst, 16)
            pe.wait_ge(l_self, 16)

            def step(s, k):
                if live(s + 1):
                    first_transposes(s + 1)
                    first_qk(s + 1)
                if live(s):
                    if isinstance(s, int) and s == 0:
                        pe.wait_ge(a_fold, 3)
                        pe.wait_ge(d_bvo, 1)
                    cross_transposes(s)
                if live(s + 1):
                    first_v(s + 1)
                if live(s):
                    cross_queries(s)
                if live(s - 1):
                    if isinstance(s, int) and s == 1:
                        pe.wait_ge(l_router, 16)
                    router_transposes(s - 1)
                    router_logits(s - 1)
                if live(s):
                    cross_scores(s, k, count(s))
                if live(s + 1):
                    first_scores(s + 1)
                if live(s):
                    cross_probs_T(s)
                    cross_z(s, k, 0)
                if live(s + 1):
                    first_probs_T(s + 1)
                if live(s):
                    cross_z(s, k, 1)
                if live(s - 1):
                    ranks(s - 1)
                if live(s + 1):
                    first_y(s + 1)
                if live(s):
                    cross_out(s)
                if isinstance(s, int) and s == -1:
                    fold_weights()

            def count(s):
                return (s // 2 + 1) * 16 if isinstance(s, int) else loop_count[0]

            loop_count = [None]

            for s in range(-1, 2):
                step(s, s % 2)
            with pe.Fori(1, NP // 2 - 1) as i:
                loop_count[0] = i * 16 + 16
                for k in range(2):
                    step(i * 2 + k, k)
            for s in range(NP - 2, NP + 1):
                step(s, s % 2)

            def tile_T(turn, k):
                wait(pe, a_eh, turn * RING + k + 1)
                wait(pe, d_ey, (turn - 1) * RING + k + 1)
                for c in range(HALF):
                    m = pe.transpose(bank[k][:, c * P:(c + 1) * P], eh[:, k, c * P:(c + 1) * P], ident)
                m.then_inc(pe_eT, 1)

            def tile_y(turn, k):
                wait(pe, a_ehT, turn * RING + k + 1)
                w = pe.value_load(tab_w[0:1, bass.ds(turn * RING + k, 1)], min_val=0, max_val=(E - 1) * HALF * D)
                for c in range(HALF):
                    m = pe.matmul(bank[k][:, D:2 * D], ehT[:, k, c], wexp[:, bass.ds(w + c * D, D)],
                                  start=(c == 0), stop=(c == HALF - 1))
                m.then_inc(pe_ey, 1)

            def turn_of_tiles(i):
                tile_T(i, 0)
                for k in range(RING):
                    if k + 1 < RING:
                        tile_T(i, k + 1)
                    tile_y(i, k)

            pe.wait_ge(l_wexp, 16)
            pe.wait_ge(d_tab, 4)
            turn_of_tiles(0)
            with pe.Fori(1, TILES // RING) as i:
                turn_of_tiles(i)

        @block.scalar
        def _(act):
            act.dma_start(wself[:, :, :, :].rearrange("p a c m -> p (a c m)"), w_self).then_inc(l_self, 16)
            act.dma_start(wfold[:, :, :, :].rearrange("p a c m -> p (a c m)"), w_fold).then_inc(l_fold, 16)
            act.dma_start(bfold[:, :], b_fold).then_inc(l_bfold, 16)

            def norm(p, n, dst, src, done, used):
                wait(act, g_rs[n], p + 1)
                wait(act, used, p)
                for g in range(G):
                    a = act.activation(dst[:, g], src(g), ACT.Identity, bias=nm[n][:, g:g + 1],
                                       scale=rs[n][:, g:g + 1])
                a.then_inc(done, 1)

            def evacuate(dst, src, ready, n_ready, used, n_used, done):
                wait(act, ready, n_ready)
                wait(act, used, n_used)
                act.activation(dst, src, ACT.Copy).then_inc(done, 1)

            def step(s, k):
                p = s + 1
                if live(p):
                    evacuate(h1T[:, :, :, :], ps_T, pe_h1T, p + 1, pe_v, p, a_h1T)
                p = s - 1
                if live(p):
                    norm(p, 2, h3, lambda g: row[:, 1 - k, g, 0:D], a_h3, pe_h3T)
                p = s
                if live(p):
                    evacuate(h2T[:, :, :, :], ps_T, pe_h2T, p + 1, pe_qt, p, a_h2T)
                p = s + 1
                if live(p):
                    for g in range(G):
                        if g == 0:
                            wait(act, pe_v, p + 1)
                            wait(act, pe_y, p)
                        a = act.activation(v[:, g].rearrange("t (i c) -> t c i", c=HALF),
                                           ps_v[:, g].rearrange("t (c i) -> t c i", c=HALF), ACT.Copy)
                    a.then_inc(a_v, 1)
                p = s
                if live(p):
                    wait(act, pe_qt, p + 1)
                    wait(act, pe_xs, p * G)
                    for c in range(HALF):
                        a = act.activation(qt[:, c], ps_qt[:, c], ACT.Identity, bias=bqk[:, c:c + 1])
                    a.then_inc(a_qt, 1)
                p = s - 1
                if live(p):
                    evacuate(h3T[:, :, :, :], ps_T, pe_h3T, p + 1, pe_lg, p, a_h3T)
                p = s
                if live(p):
                    for g in range(G):
                        wait(act, d_nbx, p * G + g + 1)
                        wait(act, pe_xpT, (p - 1) * G + g + 1)
                        if g == 0:
                            wait(act, d_rix, p)
                        act.activation(xp[:, g, 0:S], ps_xs[g], ACT.Exp, bias=nbx[:, g:g + 1], scale=SCALE,
                                       accum_out=sumx[:, g:g + 1]).then_inc(a_xp, 1)
                p = s + 1
                if live(p):
                    wait(act, d_nb1, p + 1)
                    wait(act, pe_pT, p)
                    wait(act, d_ri1, p)
                    for g in range(G):
                        act.activation(p1[:, g], sm[:, g], ACT.Exp, bias=nb1[:, g:g + 1], scale=SCALE,
                                       accum_out=sum1[:, g:g + 1]).then_inc(a_p1, 1)
                p = s
                if live(p):
                    for g in range(G):
                        evacuate(xpT[:, g], ps_xpT[g], pe_xpT, p * G + g + 1, pe_z, p, a_xpT)
                p = s + 1
                if live(p):
                    evacuate(p1T[:, :, :], ps_pT, pe_pT, p + 1, pe_y, p, a_pT)
                p = s
                if live(p):
                    evacuate(zT[:, :, :, :], ps_z, pe_z, p + 1, pe_o, p, a_z)
                p = s - 1
                if live(p):
                    wait(act, d_dif, p + 1)
                    wait(act, d_sr, p)
                    act.activation(er[:, :, :], dif[:, :, :], ACT.Exp).then_inc(a_er, 1)
                p = s + 2
                if live(p):
                    norm(p, 0, h1, lambda g: xs[:, k, g], a_h1, pe_h1T)
                p = s + 1
                if live(p):
                    norm(p, 1, h2, lambda g: x1[:, 1 - k, g], a_h2, pe_h2T)
                if isinstance(s, int) and s == -1:
                    for n, dst in ((1, wqk), (2, wvo)):
                        act.wait_ge(pe_fold, n)
                        act.activation(dst[:, :, :], bank[5 + n][:, :].rearrange("p (c d) -> p c d", c=HALF),
                                       ACT.Copy).then_inc(a_fold, 1)
                    act.wait_ge(pe_fold, 3)
                    act.activation(bqk[:, :], bank[5][:, 0:HALF], ACT.Copy).then_inc(a_fold, 1)

            norm(0, 0, h1, lambda g: xs[:, 0, g], a_h1, pe_h1T)
            steps(act, step)

            def tile_norm(turn, k, rows):
                act.wait_ge(l_rows[k], rows)
                wait(act, pe_eT, (turn - 1) * RING + k + 1)
                act.activation(eh[:, k], er_rows[:, k, 0:D], ACT.Identity, bias=er_rows[:, k, C_SHIFT:C_SHIFT + 1],
                               scale=er_rows[:, k, C_RSTD:C_RSTD + 1]).then_inc(a_eh, 1)

            def tile_T(turn, k):
                wait(act, pe_eT, turn * RING + k + 1)
                wait(act, pe_ey, (turn - 1) * RING + k + 1)
                act.activation(ehT[:, k], bank[k][:, 0:D].rearrange("p (c t) -> p c t", c=HALF), ACT.Copy
                               ).then_inc(a_ehT, 1)

            def turn_of_tiles(i, rows):
                tile_norm(i, 0, rows)
                for k in range(RING):
                    if k + 1 < RING:
                        tile_norm(i, k + 1, rows)
                    tile_T(i, k)

            turn_of_tiles(0, 16)
            with act.Fori(1, TILES // RING) as i:
                turn_of_tiles(i, i * 16 + 16)

        @block.vector
        def _(dve):
            def norm_stats(p, n, src):
                for g in range(G):
                    a = dve.bn_stats(st[n][:, g], src(g))
                a.then_inc(d_st[n], 1)
                dve.wait_ge(d_st[n], p + 1)
                dve.sem_inc(d_gate)
                for g in range(G):
                    a = dve.bn_aggr(mv[n][:, g], st[n][:, g])
                a.then_inc(d_mv[n], 1)
                dve.wait_ge(d_mv[n], p + 1)
                wait(dve, g_rs[n], p)
                dve.tensor_scalar(ve[n][:, :], mv[n][:, :, 1], EPS, None, ALU.add)
                dve.tensor_scalar(nmean[n][:, :], mv[n][:, :, 0], -1.0, None, ALU.mult).then_inc(d_ve[n], 1)

            def load_count(p, i):
                return (p // 2 + 1) * 16 if isinstance(p, int) else i

            def first_norm(p, slot, n):
                dve.wait_ge(l_x[slot], n)
                norm_stats(p, 0, lambda g: xs[:, slot, g])

            def rotate(p):
                for ps, t, ready, used, done in ((ps_q, tq, pe_q, g_q, d_tq), (ps_k, tk, pe_k, g_k, d_tk)):
                    wait(dve, ready, p + 1)
                    wait(dve, used, p)
                    dve.tensor_tensor(t[:, 0], ps, cos2.rearrange("p (c n) -> p c n", c=HALF), ALU.mult)
                    dve.tensor_tensor(t[:, 1], ps, sin2.rearrange("p (c n) -> p c n", c=HALF), ALU.mult
                                      ).then_inc(done, 1)

            def first_max(p):
                for g in range(G):
                    wait(dve, pe_s, p + 1)
                    wait(dve, a_p1, (p - 1) * G + g + 1)
                    dve.sem_inc(d_gate)
                    dve.tensor_tensor_reduce(out=sm[:, g], in0=ps_s[:, g], in1=causal, scale=1.0, scalar=-3e38,
                                             op0=ALU.add, op1=ALU.max, accum_out=mx1[:, g:g + 1]
                                             ).then_inc(d_max1, 1)
                dve.wait_ge(d_max1, (p + 1) * G)
                dve.tensor_scalar(nb1[:, :], mx1[:, :], -SCALE, None, ALU.mult).then_inc(d_nb1, 1)

            def first_sum(p):
                wait(dve, a_p1, (p + 1) * G)
                dve.reciprocal(ri1[:, :], sum1[:, :]).then_inc(d_ri1, 1)

            def first_residual(p, slot):
                dve.wait_ge(d_ri1, p + 1)
                wait(dve, pe_y, p + 1)
                wait(dve, g_x1b, p - 1)
                wait(dve, a_h2, p - 1)
                for g in range(G):
                    a = dve.scalar_tensor_tensor(out=x1[:, slot, g], in0=ps_y[:, g], scalar=ri1[:, g:g + 1],
                                                 in1=xs[:, slot, g], op0=ALU.mult, op1=ALU.add)
                a.then_inc(d_x1, 1)
                dve.wait_ge(d_x1, p + 1)
                norm_stats(p, 1, lambda g: x1[:, slot, g])

            def cross_max(p):
                for g in range(G):
                    wait(dve, pe_xs, p * G + g + 1)
                    dve.tensor_reduce(mxx[:, g:g + 1], ps_xs[g], AX.X, ALU.max).then_inc(d_maxx, 1)
                    dve.wait_ge(d_maxx, p * G + g + 1)
                    wait(dve, a_xp, (p - 1) * G + g + 1)
                    dve.tensor_scalar(nbx[:, g:g + 1], mxx[:, g:g + 1], -SCALE, None, ALU.mult).then_inc(d_nbx, 1)

            def cross_sum(p):
                wait(dve, a_xp, (p + 1) * G)
                dve.reciprocal(rix[:, :], sumx[:, :]).then_inc(d_rix, 1)

            def cross_residual(p, slot, stored):
                dve.wait_ge(d_rix, p + 1)
                wait(dve, pe_o, p + 1)
                wait(dve, g_x1b, p + 1)
                wait(dve, s_scat[slot], stored)
                for g in range(G):
                    a = dve.scalar_tensor_tensor(out=row[:, slot, g, 0:D], in0=ps_o[:, g], scalar=rix[:, g:g + 1],
                                                 in1=x1b[:, slot, g], op0=ALU.mult, op1=ALU.add)
                a.then_inc(d_x2, 1)
                dve.wait_ge(d_x2, p + 1)
                norm_stats(p, 2, lambda g: row[:, slot, g, 0:D])

            def route(p, slot):
                wait(dve, pe_lg, p + 1)
                dve.tensor_tensor(lg[:, :, :], ps_lg,
                                  wrt[0:T, HALF * E:].rearrange("t (g e) -> t g e", g=G), ALU.add).then_inc(d_lg, 1)
                dve.wait_ge(d_lg, p + 1)
                dve.tensor_reduce(mxr[:, :, :], lg[:, :, :], AX.X, ALU.max).then_inc(d_mxr, 1)
                dve.wait_ge(d_mxr, p + 1)
                wait(dve, a_er, p)
                dve.tensor_tensor(dif[:, :, :], lg[:, :, :], mxr[:, :, :].to_broadcast([T, G, E]), ALU.subtract
                                  ).then_inc(d_dif, 1)
                dve.wait_ge(d_dif, p + 1)
                dve.tensor_scalar(key[:, :, :], dif[:, :, :], 0.0, float(E), ALU.is_lt, ALU.mult).then_inc(d_key, 1)
                dve.wait_ge(d_key, p + 1)
                dve.tensor_tensor(key2[:, :, :], key[:, :, :], iota, ALU.add).then_inc(d_key2, 1)
                dve.wait_ge(d_key2, p + 1)
                dve.tensor_reduce(idx[:, :, :], key2[:, :, :], AX.X, ALU.min).then_inc(d_idx, 1)
                dve.wait_ge(d_idx, p + 1)
                wait(dve, pe_rank, p)
                dve.tensor_tensor(oh[:, :, :], iota, idx[:, :, :].to_broadcast([T, G, E]), ALU.is_equal
                                  ).then_inc(d_oh, 1)

            def route_rows(p, slot, stored):
                wait(dve, a_er, p + 1)
                dve.tensor_reduce(sr[:, :], er[:, :, :], AX.X, ALU.add).then_inc(d_sr, 1)
                dve.wait_ge(d_sr, p + 1)
                dve.reciprocal(row[:, slot, :, C_PROB], sr[:, :]).then_inc(d_w, 1)
                wait(dve, pe_rank, p + 1)
                dve.wait_ge(d_oh, p + 1)
                if not (isinstance(p, int) and p == 0):
                    dve.wait_ge(d_base, p)
                for g in range(G):
                    a = dve.tensor_tensor(rk[:, g], ps_rk[:, g], base[:, slot], ALU.add)
                dve.tensor_tensor(base[:, 1 - slot], ps_tot, base[:, slot], ALU.add).then_inc(d_base, 1)
                dve.wait_ge(d_base, p + 1)
                dve.tensor_tensor(rk2[:, :, :], rk[:, :, :], oh[:, :, :], ALU.mult).then_inc(d_rk2, 1)
                dve.wait_ge(d_rk2, p + 1)
                dve.tensor_reduce(posf[:, :], rk2[:, :, :], AX.X, ALU.add).then_inc(d_posf, 1)
                dve.wait_ge(d_posf, p + 1)
                wait(dve, s_scat[slot], stored)
                dve.tensor_copy(pos[:, slot], posf[:, :]).then_inc(d_pos, 1)

            dve.wait_ge(l_cst, 16)
            dve.tensor_copy(up[:, :], cst[0:T, K_UP:K_UP + T])
            dve.memset(ones[:, :], 1.0)
            dve.memset(xp[:, :, S:], 0.0)
            dve.tensor_copy(base[:, 0], cst[0:T, K_EXP:K_EXP + E]).then_inc(d_const, 1)
            dve.wait_ge(d_const, 1)
            first_norm(0, 0, 16)

            def step(s, k, i=None):
                if live(s - 1):
                    stored = (s - 1) // 2 * 16 * G if isinstance(s, int) else (i - 1 + k) * 16 * G
                    cross_residual(s - 1, 1 - k, stored)
                if live(s + 1):
                    rotate(s + 1)
                if live(s - 1):
                    if isinstance(s, int) and s == 1:
                        dve.wait_ge(l_router, 16)
                    route(s - 1, 1 - k)
                if live(s):
                    cross_max(s)
                if live(s + 1):
                    first_max(s + 1)
                if live(s + 2):
                    first_norm(s + 2, k, ((s + 2) // 2 + 1) * 16 if isinstance(s, int) else (i + 2) * 16)
                if live(s + 1):
                    first_sum(s + 1)
                if live(s):
                    cross_sum(s)
                if live(s - 1):
                    route_rows(s - 1, 1 - k, stored)
                if live(s + 1):
                    first_residual(s + 1, 1 - k)
                if isinstance(s, int) and s == -1:
                    dve.wait_ge(a_fold, 3)
                    dve.tensor_tensor(bvo[:, :], bank[5][0:T, D:2 * D], bfold[0:T, HALF + HALF * T:], ALU.add
                                      ).then_inc(d_bvo, 1)

            for s in range(-1, 2):
                step(s, s % 2)
            with dve.Fori(1, NP // 2 - 1) as i:
                for k in range(2):
                    step(i * 2 + k, k, i)
            for s in range(NP - 2, NP + 1):
                step(s, s % 2)

            last = NP % 2
            n = 0

            def told(a):
                nonlocal n
                n += 1
                a.then_inc(d_bvo, 1)
                dve.wait_ge(d_bvo, n + 1)

            dve.wait_ge(d_base, NP)
            told(dve.tensor_tensor(cnt[:, :], base[0:1, last], cst[0:1, K_EXP:K_EXP + E], ALU.subtract))
            c0 = cst[0:1, K_TILE:K_TILE + NTOK // P].rearrange("o (a n) -> o a n", a=1)
            told(dve.tensor_scalar(off1[0:1, 0:NTOK // P], cst[0:1, K_TILE:K_TILE + NTOK // P], float(P), None, ALU.mult))
            told(dve.tensor_tensor(big[:, :, :], cnt[:, :].rearrange("o (e a) -> o e a", a=1).to_broadcast([1, E, NTOK // P]),
                                   off1[0:1, 0:NTOK // P].rearrange("o (a n) -> o a n", a=1).to_broadcast([1, E, NTOK // P]),
                                   ALU.is_gt))
            told(dve.tensor_reduce(til[:, :], big[:, :, :], AX.X, ALU.add))
            told(dve.tensor_tensor_scan(cum[:, :], cst[0:1, K_ID:K_ID + 1].to_broadcast([1, E]), til[:, :], 0.0,
                                        ALU.mult, ALU.add))
            told(dve.tensor_tensor(ge[:, :, :],
                                   cst[0:1, K_TILE:K_TILE + TILES].rearrange("o (n a) -> o n a", a=1).to_broadcast([1, TILES, E]),
                                   cum[:, :].rearrange("o (a e) -> o a e", a=1).to_broadcast([1, TILES, E]), ALU.is_ge))
            told(dve.tensor_reduce(ex[:, :], ge[:, :, :], AX.X, ALU.add))
            told(dve.tensor_tensor(gt[:, :, :], ge[:, :, :],
                                   til[:, :].rearrange("o (a e) -> o a e", a=1).to_broadcast([1, TILES, E]), ALU.mult))
            told(dve.tensor_reduce(beg[:, :], gt[:, :, :], AX.X, ALU.add))
            told(dve.tensor_tensor(off1[:, :], cst[0:1, K_TILE:K_TILE + TILES], beg[:, :], ALU.subtract))
            told(dve.tensor_scalar(off2[:, :], off1[:, :], float(P), None, ALU.mult))
            told(dve.tensor_scalar(exc[:, :], ex[:, :], float(E - 1), None, ALU.min))
            dve.tensor_copy(tab_pad[:, :], base[0:1, last]).then_inc(d_tab, 1)
            dve.scalar_tensor_tensor(out=tab_row[:, :], in0=ex[:, :], scalar=float(CAP), in1=off2[:, :],
                                     op0=ALU.mult, op1=ALU.add).then_inc(d_tab, 1)
            dve.tensor_scalar(tab_w[:, :], exc[:, :], float(HALF * D), None, ALU.mult).then_inc(d_tab, 1)
            dve.tensor_scalar(tab_b[:, :], exc[:, :], float(D), None, ALU.mult).then_inc(d_tab, 1)
            dve.wait_ge(d_tab, 4)
            dve.wait_ge(l_bexp, 16)

            def tile(turn, k, rows):
                wait(dve, pe_ey, turn * RING + k + 1)
                b = dve.value_load(tab_b[0:1, bass.ds(turn * RING + k, 1)], min_val=0, max_val=(E - 1) * D)
                dve.tensor_tensor(ey[:, k], bank[k][:, D:2 * D], bexp[:, bass.ds(b, D)], ALU.add).then_inc(d_ey, 1)
                dve.wait_ge(d_ey, turn * RING + k + 1)
                wait(dve, s_out[k], rows - 16)
                dve.wait_ge(l_rows[k], rows)
                dve.scalar_tensor_tensor(out=eo[:, k], in0=ey[:, k], scalar=er_rows[:, k, C_PROB:C_PROB + 1],
                                         in1=er_rows[:, k, 0:D], op0=ALU.mult, op1=ALU.add).then_inc(d_eo, 1)

            for k in range(RING):
                tile(0, k, 16)
            with dve.Fori(1, TILES // RING) as i:
                for k in range(RING):
                    tile(i, k, i * 16 + 16)

        @block.gpsimd
        def _(pool):
            pool.memset(padt[:, :], 0.0).then_inc(g_const, 1)
            pool.wait_ge(g_const, 1)
            pool.memset(padt[:, C_ID:C_ID + 1].bitcast(I32), NO_TOKEN).then_inc(g_const, 1)
            pool.memset(mhalf[:, :], -0.5)
            pool.memset(step_ids[:, :], GT)
            pool.iota(row_int[:, 1, :, C_ID], pattern=[[T, G]], base=-GT, channel_multiplier=1).then_inc(g_const, 1)
            pool.wait_ge(g_const, 3)

            def powers(p, n, slot):
                wait(pool, d_ve[n], p + 1)
                used = (a_h1, a_h2, a_h3)[n]
                wait(pool, used, p)
                pool.tensor_tensor(rs[n][:, :], ve[n][:, :], mhalf[0:T, :], ALU.pow).then_inc(g_pow[n], 1)
                pool.wait_ge(g_pow[n], p + 1)
                pool.tensor_tensor(nm[n][:, :], rs[n][:, :], nmean[n][:, :], ALU.mult).then_inc(g_rs[n], 1)

            def rotated(p):
                for t, dst, ready, done in ((tq, qr, d_tq, g_q), (tk, kr, d_tk, g_k)):
                    wait(pool, ready, p + 1)
                    wait(pool, pe_s, p)
                    for c in range(HALF):
                        a = pool.tensor_tensor(dst[:, c].rearrange("p g t -> p (g t)"), t[:, 0, c], t[:, 1, 1 - c],
                                               ALU.add)
                    a.then_inc(done, 1)

            def with_bias(p, slot):
                wait(pool, d_x1, p + 1)
                wait(pool, d_x2, p - 1)
                for g in range(G):
                    a = pool.tensor_tensor(x1b[:, slot, g], x1[:, slot, g], bvo[:, :], ALU.add)
                a.then_inc(g_x1b, 1)

            def scatter(p, slot, stored):
                wait(pool, s_scat[slot], stored)
                if not (isinstance(p, int) and p == 0):
                    pool.wait_ge(g_id, p)
                pool.wait_ge(g_rs[2], p + 1)
                pool.tensor_tensor(row_int[:, slot, :, C_ID], row_int[:, 1 - slot, :, C_ID], step_ids[:, :], ALU.add)
                pool.tensor_copy(row[:, slot, :, C_RSTD], rs[2][:, :])
                pool.tensor_copy(row[:, slot, :, C_SHIFT], nm[2][:, :]).then_inc(g_id, 1)
                pool.wait_ge(g_id, p + 1)
                pool.wait_ge(d_w, p + 1)
                pool.wait_ge(d_pos, p + 1)
                pool.sem_inc(g_gate)
                for g in range(G):
                    pool.indirect_dma_start(
                        out=scratch, out_offset=bass.IndirectOffsetOnAxis(ap=pos[:, slot, g:g + 1].bitcast(U32), axis=0),
                        in_=row[:, slot, g, :], in_offset=None, bounds_check=SCR - 1, oob_is_err=False,
                    ).then_inc(s_scat[slot], 16)

            def step(s, k, i=None):
                if live(s - 1):
                    stored = (s - 1) // 2 * 16 * G if isinstance(s, int) else (i - 1 + k) * 16 * G
                    powers(s - 1, 2, 1 - k)
                if live(s + 1):
                    rotated(s + 1)
                if live(s):
                    if isinstance(s, int) and s == 0:
                        pool.wait_ge(d_bvo, 1)
                    with_bias(s, k)
                if live(s + 2):
                    powers(s + 2, 0, k)
                if live(s - 1):
                    scatter(s - 1, 1 - k, stored)
                if live(s + 1):
                    powers(s + 1, 1, 1 - k)

            powers(0, 0, 0)
            for s in range(-1, 2):
                step(s, s % 2)
            with pool.Fori(1, NP // 2 - 1) as i:
                for k in range(2):
                    step(i * 2 + k, k, i)
            for s in range(NP - 2, NP + 1):
                step(s, s % 2)

            def tile(turn, k, rows):
                pool.wait_ge(l_rows[k], rows)
                pool.wait_ge(d_eo, turn * RING + k + 1)
                pool.sem_inc(g_gate)
                pool.indirect_dma_start(
                    out=out_rows, out_offset=bass.IndirectOffsetOnAxis(ap=er_ids[:, k, C_ID:C_ID + 1], axis=0),
                    in_=eo[:, k], in_offset=None, bounds_check=NTOK - 1, oob_is_err=False,
                ).then_inc(s_out[k], 16)

            for k in range(RING):
                tile(0, k, 16)
            with pool.Fori(1, TILES // RING) as i:
                for k in range(RING):
                    tile(i, k, i * 16 + 16)


def constants():
    c = np.zeros((P, K_END), np.float32)
    c[:, K_ID:K_ID + P] = np.eye(P)
    half = D // 2
    inv = (1.0 / np.float32(10000.0) ** (np.arange(half, dtype=np.float32) / np.float32(half))).astype(np.float32)
    ang = (np.arange(T, dtype=np.float32)[None, :] * inv[:, None]).astype(np.float32)
    cos, sin = np.cos(ang).astype(np.float32), np.sin(ang).astype(np.float32)
    c[:, K_COS:K_COS + HALF * GT] = np.tile(cos, (1, HALF * G))
    c[:, K_SIN:K_SIN + GT] = np.tile(sin, (1, G))
    c[:, K_SIN + GT:K_SIN + 2 * GT] = np.tile(-sin, (1, G))
    t = np.arange(T)
    c[0:T, K_MASK:K_MASK + T] = np.where(t[None, :] <= t[:, None], 0.0, NEG)
    c[0:T, K_UP:K_UP + T] = t[:, None] < t[None, :]
    c[:, K_IOTA:K_IOTA + G * E] = np.tile(np.arange(E), G)
    c[:, K_EXP:K_EXP + E] = np.arange(E) * CAP
    c[:, K_TILE:K_TILE + TILES] = np.arange(TILES)
    return c


def by_halves(w):
    return np.ascontiguousarray(w.reshape(HALF, P, -1).transpose(1, 0, 2).reshape(P, -1))


def head_blocks(w):
    n = D // H
    full = np.zeros((HALF, n, H // HALF, n, H // HALF), w.dtype)
    for h in range(H):
        full[h % HALF, :, h // HALF, :, h // HALF] = w[:, :, h]
    return full.reshape(HALF, P, P).transpose(1, 0, 2).reshape(P, HALF * P)


def kernel(**inputs):
    import concourse.bacc as bacc
    from concourse.bass_utils import run_bass_kernel_spmd

    a = {n: np.asarray(v) for n, v in inputs.items()}
    ctx = a["ctx_1024"]
    nat = np.zeros((B, ST * P, D), ctx.dtype)
    nat[:, :S] = ctx
    nat = nat.reshape(B, ST, P, D).transpose(0, 2, 1, 3).reshape(B, P, NAT)
    trn = ctx.transpose(0, 2, 1).reshape(B, HALF, P, S).transpose(0, 2, 1, 3).reshape(B, P, TRN)
    both = np.concatenate([nat, trn], axis=2).reshape(NP, G, P, CW).transpose(0, 2, 1, 3).reshape(NP * P, G * CW)
    w_fold = np.concatenate([by_halves(a["L0_xattn_Wq"]), by_halves(a["L0_xattn_Wk"]), by_halves(a["L0_xattn_Wv"]),
                             by_halves(a["L0_xattn_Wo"].T)], axis=1)
    bv = np.repeat(a["L0_xattn_bv"].reshape(HALF, P).T, T, axis=1)
    b_fold = np.concatenate([a["L0_xattn_bq"].reshape(HALF, P).T, bv, np.tile(a["L0_xattn_bo"], (P, 1))], axis=1)
    w_router = np.concatenate([by_halves(a["L0_ffn_router_w"].T), np.tile(a["L0_ffn_router_b"], (P, G))], axis=1)
    w_expert = a["L0_ffn_expert_w"].transpose(0, 2, 1).reshape(E, HALF, P, D).transpose(2, 0, 1, 3).reshape(P, -1)
    arrays = {
        "x": a["x"], "ctxs": both, "consts": constants(),
        "w_self": np.concatenate([head_blocks(a[f"L0_attn_w_{n}"]) for n in "qkv"], axis=1),
        "w_fold": w_fold, "b_fold": b_fold, "w_router": w_router, "w_expert": w_expert,
        "b_expert": np.tile(a["L0_ffn_expert_b"].reshape(1, -1), (P, 1)),
    }
    arrays = {f"in_{n}": np.ascontiguousarray(v) for n, v in arrays.items()}
    nc = bacc.Bacc("TRN2", target_bir_lowering=False, num_devices=1)
    args = [nc.dram_tensor(n, v.shape, mybir.dt.from_np(v.dtype), kind="ExternalInput").ap()
            for n, v in arrays.items()]
    out = nc.dram_tensor("out", (B, T, D), F32, kind="ExternalOutput").ap()
    build(nc, *args, out)
    return run_bass_kernel_spmd(nc, [arrays], core_ids=[0]).results[0]["out"]
```

```python
from contextlib import ExitStack

import numpy as np

import concourse.bass as bass
from concourse import mybir

F32 = mybir.dt.float32
BF16 = mybir.dt.bfloat16
I32 = mybir.dt.int32
U32 = mybir.dt.uint32
ALU = mybir.AluOpType
ACT = mybir.ActivationFunctionType
AX = mybir.AxisListType

B, T, D = 32, 112, 256
S = 375
H = 16
E = 8
P = 128
G = 2
NP = B // G
GT = G * T
HALF = D // P
ST = -(-S // P)
NAT = ST * D
TRN = HALF * S
CW = NAT + TRN
SCALE = float(D) ** -0.5
EPS = 1e-5
NEG = -1e30

C_RSTD, C_SHIFT, C_PROB, C_ID, ROW = D, D + 1, D + 2, D + 3, D + 4
NTOK = B * T
CAP = NTOK + P
TILES = NTOK // P + E - 1
IDLE = E - 1
SCR = E * CAP + IDLE * P
NO_TOKEN = 1 << 20
RING = 7

K_ID, K_COS, K_SIN, K_MASK, K_UP, K_IOTA, K_EXP, K_TILE = np.cumsum(
    [0, P, HALF * GT, HALF * GT, T, T, G * E, E]).tolist()
K_END = K_TILE + TILES + 1


def wait(eng, sem, n):
    if isinstance(n, int) and n <= 0:
        return
    eng.wait_ge(sem, n)


def build(nc, x, ctxs, consts, w_self, w_fold, b_fold, w_router, w_expert, b_expert, out):
    with ExitStack() as stack:
        def sb(name, shape, dt=F32):
            return stack.enter_context(nc.sbuf_tensor(name, shape, dt))

        def sem(name):
            return stack.enter_context(nc.semaphore(name))

        scratch = nc.dram_tensor("routed_rows", (SCR, ROW), F32).ap()
        x_rows = x.rearrange("b t d -> (b t) d")
        out_rows = out.rearrange("b t d -> (b t) d")

        cst = sb("cst", [P, K_END])
        ident = cst[:, K_ID:K_ID + P]
        cos2 = cst[:, K_COS:K_COS + HALF * GT]
        sin2 = cst[:, K_SIN:K_SIN + HALF * GT]
        causal = cst[0:T, K_MASK:K_MASK + T]
        iota = cst[0:T, K_IOTA:K_IOTA + G * E].rearrange("t (g e) -> t g e", g=G)
        up = sb("up", [T, T], BF16)
        ones = sb("ones", [T, T], BF16)
        wself = sb("wself", [P, 3, HALF, P])
        wfold = sb("wfold", [P, 4, HALF, D])
        bfold = sb("bfold", [P, HALF + HALF * T + D])
        wqk = sb("wqk", [P, HALF, D])
        wvo = sb("wvo", [P, HALF, D])
        bqk = sb("bqk", [P, HALF])
        bvo = sb("bvo", [T, D])
        wrt = sb("wrt", [P, HALF * E + G * E])
        wexp = sb("wexp", [P, E * HALF * D])
        bexp = sb("bexp", [P, E * D])
        padt = sb("padt", [P, ROW])
        mhalf = sb("mhalf", [P, G])
        step_ids = sb("step_ids", [T, G], I32)

        xs = sb("xs", [T, 2, G, D])
        h1 = sb("h1", [T, G, D])
        h1T = sb("h1T", [P, HALF, G, T])
        tq = sb("tq", [P, 2, HALF, GT])
        tk = sb("tk", [P, 2, HALF, GT])
        qr = sb("qr", [P, HALF, G, T])
        kr = sb("kr", [P, HALF, G, T])
        v = sb("v", [T, G, D])
        sm = sb("sm", [T, G, T])
        p1 = sb("p1", [T, G, T])
        p1T = sb("p1T", [T, G, T])
        mx1 = sb("mx1", [T, G])
        nb1 = sb("nb1", [T, G])
        sum1 = sb("sum1", [T, G])
        ri1 = sb("ri1", [T, G])
        cx = sb("cx", [P, 2, G, CW])
        x1 = sb("x1", [T, 2, G, D])
        x1b = sb("x1b", [T, 2, G, D])
        h2 = sb("h2", [T, G, D])
        h2T = sb("h2T", [P, HALF, G, T])
        qt = sb("qt", [P, HALF, G, T])
        xp = sb("xp", [T, G, ST * P])
        xpT = sb("xpT", [P, G, ST, T])
        zT = sb("zT", [P, HALF, G, T])
        mxx = sb("mxx", [T, G])
        nbx = sb("nbx", [T, G])
        sumx = sb("sumx", [T, G])
        rix = sb("rix", [T, G])
        row = sb("row", [T, 2, G, ROW])
        row_int = row[:, :, :, :].bitcast(I32)
        h3 = sb("h3", [T, G, D])
        h3T = sb("h3T", [P, HALF, G, T])
        lg = sb("lg", [T, G, E])
        mxr = sb("mxr", [T, G, 1])
        dif = sb("dif", [T, G, E])
        er = sb("er", [T, G, E])
        sr = sb("sr", [T, G])
        key = sb("key", [T, G, E])
        key2 = sb("key2", [T, G, E])
        idx = sb("idx", [T, G, 1])
        oh = sb("oh", [T, G, E], BF16)
        rk = sb("rk", [T, G, E])
        rk2 = sb("rk2", [T, G, E])
        base = sb("base", [T, 2, E])
        posf = sb("posf", [T, G])
        pos = sb("pos", [T, 2, G], I32)
        st = [sb(f"st{n}", [T, G, 6]) for n in range(3)]
        mv = [sb(f"mv{n}", [T, G, 2]) for n in range(3)]
        ve = [sb(f"ve{n}", [T, G]) for n in range(3)]
        nmean = [sb(f"nmean{n}", [T, G]) for n in range(3)]
        rs = {(n, k): sb(f"rs{n}{k}", [T, G]) for n in range(2) for k in range(2)}
        nm = {(n, k): sb(f"nm{n}{k}", [T, G]) for n in range(2) for k in range(2)}
        for k in range(2):
            rs[2, k], nm[2, k] = row[:, k, :, C_RSTD], row[:, k, :, C_SHIFT]
        cnt = sb("cnt", [1, E])
        big = sb("big", [1, E, NTOK // P])
        til = sb("til", [1, E])
        cum = sb("cum", [1, E])
        ge = sb("ge", [1, TILES, E])
        gt = sb("gt", [1, TILES, E])
        ex = sb("ex", [1, TILES])
        beg = sb("beg", [1, TILES])
        off1 = sb("off1", [1, TILES])
        off2 = sb("off2", [1, TILES])
        exc = sb("exc", [1, TILES])
        tab_row = sb("tab_row", [1, TILES], I32)
        tab_w = sb("tab_w", [1, TILES], I32)
        tab_b = sb("tab_b", [1, TILES], I32)
        tab_pad = sb("tab_pad", [1, E], I32)
        er_rows = sb("er_rows", [P, RING, ROW])
        er_ids = er_rows[:, :, :].bitcast(U32)
        eid = sb("eid", [P, RING], U32)
        eh = sb("eh", [P, RING, D])
        ehT = sb("ehT", [P, RING, HALF, P])
        ey = sb("ey", [P, RING, D])
        eo = sb("eo", [P, RING, D])

        bank = [stack.enter_context(nc.psum_tensor(f"bank{n}", [P, 512], F32)) for n in range(8)]
        ps_T = bank[0][:, 0:HALF * GT].rearrange("p (c g t) -> p c g t", c=HALF, g=G)
        ps_q = bank[1][:, 0:HALF * GT].rearrange("p (c n) -> p c n", c=HALF)
        ps_k = bank[2][:, 0:HALF * GT].rearrange("p (c n) -> p c n", c=HALF)
        ps_v = bank[3][0:T, :].rearrange("t (g d) -> t g d", g=G)
        ps_y = ps_v
        ps_s = bank[4][0:T, 0:GT].rearrange("t (g k) -> t g k", g=G)
        ps_pT = bank[4][0:T, GT:2 * GT].rearrange("t (g k) -> t g k", g=G)
        ps_lg = bank[4][0:T, 2 * GT:2 * GT + G * E].rearrange("t (g e) -> t g e", g=G)
        ps_rk = bank[1][0:T, 2 * GT:2 * GT + G * E].rearrange("t (g e) -> t g e", g=G)
        ps_tot = bank[1][0:T, 2 * GT + G * E:2 * GT + G * E + E]
        ps_qt = [bank[n][:, 0:GT].rearrange("p (g t) -> p g t", g=G) for n in (5, 0)]
        ps_z = bank[5][:, 0:HALF * GT].rearrange("p (c g t) -> p c g t", c=HALF, g=G)
        ps_xs = [bank[6 + g][0:T, 0:S] for g in range(G)]
        ps_xpT = [bank[6 + g][:, 0:ST * T].rearrange("p (n t) -> p n t", n=ST) for g in range(G)]
        ps_o = bank[6][0:T, :].rearrange("t (g d) -> t g d", g=G)

        l_cst, l_self, l_fold, l_bfold, l_router, l_wexp, l_bexp = (
            sem(n) for n in ("l_cst", "l_self", "l_fold", "l_bfold", "l_router", "l_wexp", "l_bexp"))
        l_x = [sem(f"l_x{n}") for n in range(2)]
        l_cx = [sem(f"l_cx{n}") for n in range(2)]
        s_scat = [sem(f"s_scat{n}") for n in range(2)]
        s_pad = sem("s_pad")
        l_rows = [sem(f"l_rows{n}") for n in range(RING)]
        s_out = [sem(f"s_out{n}") for n in range(RING)]
        (pe_h1T, pe_q, pe_k, pe_v, pe_s, pe_pT, pe_y, pe_h2T, pe_qt, pe_xs, pe_xpT, pe_z, pe_o, pe_h3T,
         pe_lg, pe_rank, pe_fold, pe_eT, pe_ey) = (sem(n) for n in (
            "pe_h1T pe_q pe_k pe_v pe_s pe_pT pe_y pe_h2T pe_qt pe_xs pe_xpT pe_z pe_o pe_h3T "
            "pe_lg pe_rank pe_fold pe_eT pe_ey").split())
        (a_h1, a_h1T, a_v, a_p1, a_pT, a_h2, a_h2T, a_qt, a_xp, a_xpT, a_z, a_h3, a_h3T, a_er, a_fold,
         a_eh, a_ehT) = (sem(n) for n in (
            "a_h1 a_h1T a_v a_p1 a_pT a_h2 a_h2T a_qt a_xp a_xpT a_z a_h3 a_h3T a_er a_fold "
            "a_eh a_ehT").split())
        (d_tq, d_tk, d_max1, d_nb1, d_ri1, d_x1, d_maxx, d_nbx, d_rix, d_x2, d_lg, d_mxr, d_dif, d_sr, d_w,
         d_key, d_key2, d_idx, d_oh, d_rk2, d_posf, d_pos, d_base, d_bvo, d_tab, d_ey, d_eo) = (sem(n) for n in (
            "d_tq d_tk d_max1 d_nb1 d_ri1 d_x1 d_maxx d_nbx d_rix d_x2 d_lg d_mxr d_dif d_sr d_w "
            "d_key d_key2 d_idx d_oh d_rk2 d_posf d_pos d_base d_bvo d_tab d_ey d_eo").split())
        d_st = [sem(f"d_st{n}") for n in range(3)]
        d_mv = [sem(f"d_mv{n}") for n in range(3)]
        d_ve = [sem(f"d_ve{n}") for n in range(3)]
        g_const, g_q, g_k, g_x1b, g_id = (sem(n) for n in "g_const g_q g_k g_x1b g_id".split())
        d_gate, g_gate = sem("d_gate"), sem("g_gate")
        g_pow = [sem(f"g_pow{n}") for n in range(3)]
        g_rs = [sem(f"g_rs{n}") for n in range(3)]

        def live(p):
            return not isinstance(p, int) or 0 <= p < NP

        def steps(eng, step):
            for s in range(-2, 2):
                step(s, s % 2, s // 2)
            with eng.Fori(1, NP // 2 - 1) as i:
                for k in range(2):
                    step(i * 2 + k, k, i)
            for s in range(NP - 2, NP + 2):
                step(s, s % 2, s // 2)

        block = stack.enter_context(nc.Block())

        @block.sync
        def _(sp):
            def load_x(p, slot):
                wait(sp, d_x1, p - 1)
                sp.dma_start(xs[:, slot], x_rows[bass.ds(p * GT, GT), :].rearrange("(g t) d -> t g d", g=G)
                             ).then_inc(l_x[slot], 16)

            def load_ctx(p, slot):
                wait(sp, pe_z, p - 1)
                sp.dma_start(cx[:, slot].rearrange("p g c -> p (g c)"), ctxs[bass.ds(p * P, P), :]
                             ).then_inc(l_cx[slot], 16)

            def step(s, k, half):
                if live(s + 2) and not (isinstance(s, int) and s == -2):
                    load_x(s + 2, k)
                if isinstance(s, int) and s == -1:
                    sp.dma_start(wrt[:, :], w_router).then_inc(l_router, 16)
                if live(s + 1):
                    load_ctx(s + 1, 1 - k)
                if isinstance(s, int) and s == 0:
                    sp.dma_start(wexp[:, :], w_expert).then_inc(l_wexp, 16)
                    sp.dma_start(bexp[:, :], b_expert).then_inc(l_bexp, 16)

            load_x(0, 0)
            sp.dma_start(cst[:, :], consts).then_inc(l_cst, 16)
            steps(sp, step)

            sp.wait_ge(d_tab, 4)
            for n in range(2):
                sp.wait_ge(s_scat[n], 16 + 16 * G * NP // 2)
            for e in range(E):
                r = sp.value_load(tab_pad[0:1, e:e + 1], min_val=e * CAP, max_val=e * CAP + NTOK)
                sp.dma_start(scratch[bass.ds(r, P), :], padt[:, :]).then_inc(s_pad, 16)
            sp.wait_ge(s_pad, 16 * E)

            def tile(j, k, turn):
                wait(sp, d_eo, (turn - 1) * RING + k + 1)
                r = sp.value_load(tab_row[0:1, bass.ds(j, 1)], min_val=0, max_val=SCR - P)
                sp.dma_start(er_rows[:, k, :], scratch[bass.ds(r, P), :]).then_inc(l_rows[k], 16)

            for k in range(RING):
                tile(k, k, 0)
            with sp.Fori(1, TILES // RING) as i:
                for k in range(RING):
                    tile(i * RING + k, k, i)
            for k in range(RING):
                sp.wait_ge(s_out[k], 16 * (TILES // RING))

        @block.tensor
        def _(pe):
            def first_transposes(p):
                wait(pe, a_h1, p + 1)
                wait(pe, a_qt, (p - 1) * HALF)
                for c in range(HALF):
                    for g in range(G):
                        m = pe.transpose(ps_T[:, c, g], h1[:, g, c::2], ident[0:T, 0:T])
                m.then_inc(pe_h1T, 1)

            def first_qk(p):
                wait(pe, a_h1T, p + 1)
                for n, (ps, ready, used) in enumerate(((ps_q, pe_q, d_tq), (ps_k, pe_k, d_tk))):
                    wait(pe, used, p)
                    if n == 0:
                        wait(pe, d_base, p - 2)
                    for c in range(HALF):
                        m = pe.matmul(ps[:, c], wself[:, n, c], h1T[:, c].rearrange("p g t -> p (g t)"),
                                      start=True, stop=True)
                    m.then_inc(ready, 1)

            def first_v(p):
                wait(pe, d_x1, p)
                for g in range(G):
                    for c in range(HALF):
                        m = pe.matmul(ps_v[:, g, c * P:(c + 1) * P], h1T[:, c, g], wself[:, 2, c],
                                      start=True, stop=True)
                m.then_inc(pe_v, 1)

            def first_scores(p):
                wait(pe, g_q, p + 1)
                wait(pe, g_k, p + 1)
                wait(pe, d_max1, p * G)
                wait(pe, d_lg, p - 2)
                for g in range(G):
                    for c in range(HALF):
                        m = pe.matmul(ps_s[:, g], qr[:, c, g], kr[:, c, g], start=(c == 0), stop=(c == HALF - 1))
                m.then_inc(pe_s, 1)

            def first_probs_T(p):
                wait(pe, a_p1, (p + 1) * G)
                for g in range(G):
                    m = pe.transpose(ps_pT[:, g], p1[:, g], ident[0:T, 0:T])
                m.then_inc(pe_pT, 1)

            def first_y(p):
                wait(pe, a_v, p + 1)
                wait(pe, a_pT, p + 1)
                for g in range(G):
                    m = pe.matmul(ps_y[:, g], p1T[:, g], v[:, g], start=True, stop=True)
                m.then_inc(pe_y, 1)

            def cross_transposes(p):
                wait(pe, a_h2, p + 1)
                wait(pe, a_h3T, p - 1)
                for c in range(HALF):
                    for g in range(G):
                        m = pe.transpose(ps_T[:, c, g], h2[:, g, c * P:(c + 1) * P], ident[0:T, 0:T])
                m.then_inc(pe_h2T, 1)

            def cross_queries(p):
                wait(pe, a_h2T, p + 1)
                wait(pe, a_z, p)
                for c in range(HALF):
                    for n in range(HALF):
                        m = pe.matmul(ps_qt[c].rearrange("p g t -> p (g t)"), wqk[:, n, c * P:(c + 1) * P],
                                      h2T[:, n].rearrange("p g t -> p (g t)"), start=(n == 0), stop=(n == HALF - 1))
                    m.then_inc(pe_qt, 1)

            def cross_scores(p, slot, half, g):
                if g == 0:
                    pe.wait_ge(l_cx[slot], half * 16 + 16)
                    wait(pe, d_x2, p)
                wait(pe, a_xpT, (p - 1) * G + g + 1)
                for c in range(HALF):
                    if g == 0:
                        wait(pe, a_qt, p * HALF + c + 1)
                    m = pe.matmul(ps_xs[g], qt[:, c, g], cx[:, slot, g, NAT + c * S:NAT + (c + 1) * S],
                                  start=(c == 0), stop=(c == HALF - 1))
                m.then_inc(pe_xs, 1)

            def cross_probs_T(p):
                for g in range(G):
                    wait(pe, a_xp, p * G + g + 1)
                    for n in range(ST):
                        m = pe.transpose(ps_xpT[g][:, n], xp[:, g, n * P:(n + 1) * P], ident[0:T, 0:T])
                    m.then_inc(pe_xpT, 1)

            def cross_z(p, slot, g):
                wait(pe, a_xpT, p * G + g + 1)
                for c in range(HALF):
                    for n in range(ST):
                        m = pe.matmul(ps_z[:, c, g], cx[:, slot, g, n * D + c * P:n * D + (c + 1) * P],
                                      xpT[:, g, n], start=(n == 0), stop=(n == ST - 1))
                if g == G - 1:
                    m.then_inc(pe_z, 1)

            def cross_out(p):
                wait(pe, a_z, p + 1)
                for g in range(G):
                    for c in range(HALF):
                        m = pe.matmul(ps_o[:, g], zT[:, c, g], wvo[:, c], start=(c == 0), stop=(c == HALF - 1))
                m.then_inc(pe_o, 1)

            def router_transposes(p):
                wait(pe, a_h3, p + 1)
                if live(p + 3):
                    wait(pe, a_h1T, p + 4)
                else:
                    wait(pe, a_qt, min(p + 2, NP) * HALF)
                for c in range(HALF):
                    for g in range(G):
                        m = pe.transpose(ps_T[:, c, g], h3[:, g, c * P:(c + 1) * P], ident[0:T, 0:T])
                m.then_inc(pe_h3T, 1)

            def router_logits(p):
                wait(pe, a_h3T, p + 1)
                if live(p + 2):
                    wait(pe, a_pT, p + 3)
                for g in range(G):
                    for c in range(HALF):
                        m = pe.matmul(ps_lg[:, g], h3T[:, c, g], wrt[:, c * E:(c + 1) * E],
                                      start=(c == 0), stop=(c == HALF - 1))
                m.then_inc(pe_lg, 1)

            def ranks(p):
                wait(pe, d_oh, p + 1)
                if live(p + 3):
                    wait(pe, d_tq, p + 4)
                pe.matmul(ps_rk[:, 0], up[:, :], oh[:, 0], start=True, stop=True)
                pe.matmul(ps_rk[:, 1], up[:, :], oh[:, 1], start=True, stop=False)
                pe.matmul(ps_rk[:, 1], ones[:, :], oh[:, 0], start=False, stop=True)
                pe.matmul(ps_tot, ones[:, :], oh[:, 0], start=True, stop=False)
                pe.matmul(ps_tot, ones[:, :], oh[:, 1], start=False, stop=True).then_inc(pe_rank, 1)

            def fold_weights():
                pe.wait_ge(l_fold, 16)
                pe.wait_ge(l_bfold, 16)
                for n, (a, b, ps) in enumerate(((0, 1, bank[6]), (2, 3, bank[7]))):
                    for c in range(HALF):
                        for e in range(HALF):
                            m = pe.matmul(ps[:, c * D:(c + 1) * D], wfold[:, a, e, c * P:(c + 1) * P],
                                          wfold[:, b, e, :], start=(e == 0), stop=(e == HALF - 1))
                    m.then_inc(pe_fold, 1)
                for c in range(HALF):
                    for e in range(HALF):
                        pe.matmul(bank[5][:, c:c + 1], wfold[:, 1, e, c * P:(c + 1) * P], bfold[:, e:e + 1],
                                  start=(e == 0), stop=(e == HALF - 1))
                for e in range(HALF):
                    m = pe.matmul(bank[5][0:T, D:2 * D], bfold[:, HALF + e * T:HALF + (e + 1) * T],
                                  wfold[:, 3, e, :], start=(e == 0), stop=(e == HALF - 1))
                m.then_inc(pe_fold, 1)

            pe.wait_ge(l_cst, 16)
            pe.wait_ge(l_self, 16)

            def step(s, k, half):
                if live(s):
                    if isinstance(s, int) and s == 0:
                        pe.wait_ge(a_fold, 3)
                        pe.wait_ge(d_bvo, 1)
                    cross_transposes(s)
                if live(s - 2):
                    ranks(s - 2)
                if live(s + 1):
                    first_scores(s + 1)
                if live(s):
                    cross_queries(s)
                    cross_scores(s, k, half, 0)
                if live(s + 1):
                    first_probs_T(s + 1)
                if live(s):
                    cross_scores(s, k, half, 1)
                if live(s + 2):
                    first_transposes(s + 2)
                if live(s + 1):
                    first_y(s + 1)
                if live(s):
                    cross_probs_T(s)
                if live(s + 2):
                    first_qk(s + 2)
                if live(s):
                    for g in range(G):
                        cross_z(s, k, g)
                if live(s - 1):
                    if isinstance(s, int) and s == 1:
                        pe.wait_ge(l_router, 16)
                    router_transposes(s - 1)
                if live(s + 2):
                    first_v(s + 2)
                if live(s - 1):
                    router_logits(s - 1)
                if live(s):
                    cross_out(s)
                if isinstance(s, int) and s == -2:
                    fold_weights()

            steps(pe, step)

            def tile_T(turn, k):
                wait(pe, a_eh, turn * RING + k + 1)
                wait(pe, d_ey, (turn - 1) * RING + k + 1)
                for c in range(HALF):
                    m = pe.transpose(bank[k][:, c * P:(c + 1) * P], eh[:, k, c * P:(c + 1) * P], ident)
                m.then_inc(pe_eT, 1)

            def tile_y(turn, k):
                wait(pe, a_ehT, turn * RING + k + 1)
                w = pe.value_load(tab_w[0:1, bass.ds(turn * RING + k, 1)], min_val=0, max_val=(E - 1) * HALF * D)
                for c in range(HALF):
                    m = pe.matmul(bank[k][:, D:2 * D], ehT[:, k, c], wexp[:, bass.ds(w + c * D, D)],
                                  start=(c == 0), stop=(c == HALF - 1))
                m.then_inc(pe_ey, 1)

            def turn_of_tiles(i):
                tile_T(i, 0)
                for k in range(RING):
                    if k + 1 < RING:
                        tile_T(i, k + 1)
                    tile_y(i, k)

            pe.wait_ge(l_wexp, 16)
            pe.wait_ge(d_tab, 4)
            turn_of_tiles(0)
            with pe.Fori(1, TILES // RING) as i:
                turn_of_tiles(i)

        @block.scalar
        def _(act):
            act.dma_start(wself[:, :, :, :].rearrange("p a c m -> p (a c m)"), w_self).then_inc(l_self, 16)
            act.dma_start(wfold[:, :, :, :].rearrange("p a c m -> p (a c m)"), w_fold).then_inc(l_fold, 16)
            act.dma_start(bfold[:, :], b_fold).then_inc(l_bfold, 16)

            def norm(p, n, slot, dst, src, done, used):
                wait(act, g_rs[n], p + 1)
                wait(act, used, p)
                for g in range(G):
                    a = act.activation(dst[:, g], src(g), ACT.Identity, bias=nm[n, slot][:, g:g + 1],
                                       scale=rs[n, slot][:, g:g + 1])
                a.then_inc(done, 1)

            def evacuate(dst, src, ready, n_ready, used, n_used, done):
                wait(act, ready, n_ready)
                wait(act, used, n_used)
                act.activation(dst, src, ACT.Copy).then_inc(done, 1)

            def step(s, k, half):
                p = s
                if live(p):
                    evacuate(h2T[:, :, :, :], ps_T, pe_h2T, p + 1, pe_qt, p * HALF, a_h2T)
                    for c in range(HALF):
                        wait(act, pe_qt, p * HALF + c + 1)
                        wait(act, pe_xs, p * G)
                        act.activation(qt[:, c], ps_qt[c], ACT.Identity, bias=bqk[:, c:c + 1]).then_inc(a_qt, 1)
                p = s + 1
                if live(p):
                    wait(act, d_nb1, p + 1)
                    wait(act, pe_pT, p)
                    wait(act, d_ri1, p)
                    for g in range(G):
                        act.activation(p1[:, g], sm[:, g], ACT.Exp, bias=nb1[:, g:g + 1], scale=SCALE,
                                       accum_out=sum1[:, g:g + 1]).then_inc(a_p1, 1)
                p = s + 2
                if live(p):
                    norm(p, 0, k, h1, lambda g: xs[:, k, g], a_h1, pe_h1T)
                for g in range(G):
                    if live(s):
                        wait(act, d_nbx, s * G + g + 1)
                        wait(act, pe_xpT, (s - 1) * G + g + 1)
                        if g == 0:
                            wait(act, d_rix, s)
                        act.activation(xp[:, g, 0:S], ps_xs[g], ACT.Exp, bias=nbx[:, g:g + 1], scale=SCALE,
                                       accum_out=sumx[:, g:g + 1]).then_inc(a_xp, 1)
                    p = s + 1
                    if g == 0 and live(p):
                        evacuate(p1T[:, :, :], ps_pT, pe_pT, p + 1, pe_y, p, a_pT)
                p = s + 2
                if live(p):
                    evacuate(h1T[:, :, :, :], ps_T, pe_h1T, p + 1, pe_v, p, a_h1T)
                p = s
                if live(p):
                    for g in range(G):
                        evacuate(xpT[:, g], ps_xpT[g], pe_xpT, p * G + g + 1, pe_z, p, a_xpT)
                p = s - 1
                if live(p):
                    norm(p, 2, 1 - k, h3, lambda g: row[:, 1 - k, g, 0:D], a_h3, pe_h3T)
                p = s + 1
                if live(p):
                    norm(p, 1, 1 - k, h2, lambda g: x1[:, 1 - k, g], a_h2, pe_h2T)
                p = s
                if live(p):
                    evacuate(zT[:, :, :, :], ps_z, pe_z, p + 1, pe_o, p, a_z)
                p = s - 1
                if live(p):
                    evacuate(h3T[:, :, :, :], ps_T, pe_h3T, p + 1, pe_lg, p, a_h3T)
                p = s + 2
                if live(p):
                    wait(act, pe_v, p + 1)
                    wait(act, pe_y, p)
                    for g in range(G):
                        a = act.activation(v[:, g].rearrange("t (i c) -> t c i", c=HALF),
                                           ps_v[:, g].rearrange("t (c i) -> t c i", c=HALF), ACT.Copy)
                    a.then_inc(a_v, 1)
                p = s - 1
                if live(p):
                    wait(act, d_dif, p + 1)
                    wait(act, d_sr, p)
                    act.activation(er[:, :, :], dif[:, :, :], ACT.Exp).then_inc(a_er, 1)
                if isinstance(s, int) and s == -2:
                    for n, dst in ((1, wqk), (2, wvo)):
                        act.wait_ge(pe_fold, n)
                        act.activation(dst[:, :, :], bank[5 + n][:, :].rearrange("p (c d) -> p c d", c=HALF),
                                       ACT.Copy).then_inc(a_fold, 1)
                    act.wait_ge(pe_fold, 3)
                    act.activation(bqk[:, :], bank[5][:, 0:HALF], ACT.Copy).then_inc(a_fold, 1)

            steps(act, step)

            def tile_norm(turn, k, rows):
                act.wait_ge(l_rows[k], rows)
                wait(act, pe_eT, (turn - 1) * RING + k + 1)
                act.activation(eh[:, k], er_rows[:, k, 0:D], ACT.Identity, bias=er_rows[:, k, C_SHIFT:C_SHIFT + 1],
                               scale=er_rows[:, k, C_RSTD:C_RSTD + 1]).then_inc(a_eh, 1)

            def tile_T(turn, k):
                wait(act, pe_eT, turn * RING + k + 1)
                wait(act, pe_ey, (turn - 1) * RING + k + 1)
                act.activation(ehT[:, k], bank[k][:, 0:D].rearrange("p (c t) -> p c t", c=HALF), ACT.Copy
                               ).then_inc(a_ehT, 1)

            def turn_of_tiles(i, rows):
                tile_norm(i, 0, rows)
                for k in range(RING):
                    if k + 1 < RING:
                        tile_norm(i, k + 1, rows)
                    tile_T(i, k)

            turn_of_tiles(0, 16)
            with act.Fori(1, TILES // RING) as i:
                turn_of_tiles(i, i * 16 + 16)

        @block.vector
        def _(dve):
            def norm_stats(p, n, src):
                for g in range(G):
                    a = dve.bn_stats(st[n][:, g], src(g))
                a.then_inc(d_st[n], 1)
                dve.wait_ge(d_st[n], p + 1)
                dve.sem_inc(d_gate)
                for g in range(G):
                    a = dve.bn_aggr(mv[n][:, g], st[n][:, g])
                a.then_inc(d_mv[n], 1)
                dve.wait_ge(d_mv[n], p + 1)
                wait(dve, g_rs[n], p)
                dve.tensor_scalar(ve[n][:, :], mv[n][:, :, 1], EPS, None, ALU.add)
                dve.tensor_scalar(nmean[n][:, :], mv[n][:, :, 0], -1.0, None, ALU.mult).then_inc(d_ve[n], 1)

            def first_norm(p, slot, n):
                dve.wait_ge(l_x[slot], n)
                norm_stats(p, 0, lambda g: xs[:, slot, g])

            def rotate(p):
                for ps, t, ready, used, done in ((ps_q, tq, pe_q, g_q, d_tq), (ps_k, tk, pe_k, g_k, d_tk)):
                    wait(dve, ready, p + 1)
                    wait(dve, used, p)
                    dve.tensor_tensor(t[:, 0], ps, cos2.rearrange("p (c n) -> p c n", c=HALF), ALU.mult)
                    dve.tensor_tensor(t[:, 1], ps, sin2.rearrange("p (c n) -> p c n", c=HALF), ALU.mult
                                      ).then_inc(done, 1)

            def first_max(p):
                for g in range(G):
                    wait(dve, pe_s, p + 1)
                    wait(dve, a_p1, (p - 1) * G + g + 1)
                    dve.sem_inc(d_gate)
                    dve.tensor_tensor_reduce(out=sm[:, g], in0=ps_s[:, g], in1=causal, scale=1.0, scalar=-3e38,
                                             op0=ALU.add, op1=ALU.max, accum_out=mx1[:, g:g + 1]
                                             ).then_inc(d_max1, 1)
                dve.wait_ge(d_max1, (p + 1) * G)
                dve.tensor_scalar(nb1[:, :], mx1[:, :], -SCALE, None, ALU.mult).then_inc(d_nb1, 1)

            def first_sum(p):
                wait(dve, a_p1, (p + 1) * G)
                dve.reciprocal(ri1[:, :], sum1[:, :]).then_inc(d_ri1, 1)

            def first_residual(p, slot):
                dve.wait_ge(d_ri1, p + 1)
                wait(dve, pe_y, p + 1)
                wait(dve, g_x1b, p - 1)
                wait(dve, a_h2, p - 1)
                for g in range(G):
                    a = dve.scalar_tensor_tensor(out=x1[:, slot, g], in0=ps_y[:, g], scalar=ri1[:, g:g + 1],
                                                 in1=xs[:, slot, g], op0=ALU.mult, op1=ALU.add)
                a.then_inc(d_x1, 1)
                dve.wait_ge(d_x1, p + 1)
                norm_stats(p, 1, lambda g: x1[:, slot, g])

            def cross_max(p, g):
                wait(dve, pe_xs, p * G + g + 1)
                dve.tensor_reduce(mxx[:, g:g + 1], ps_xs[g], AX.X, ALU.max).then_inc(d_maxx, 1)
                dve.wait_ge(d_maxx, p * G + g + 1)
                wait(dve, a_xp, (p - 1) * G + g + 1)
                dve.tensor_scalar(nbx[:, g:g + 1], mxx[:, g:g + 1], -SCALE, None, ALU.mult).then_inc(d_nbx, 1)

            def cross_sum(p):
                wait(dve, a_xp, (p + 1) * G)
                dve.reciprocal(rix[:, :], sumx[:, :]).then_inc(d_rix, 1)

            def cross_residual(p, slot, stored):
                dve.wait_ge(d_rix, p + 1)
                wait(dve, pe_o, p + 1)
                wait(dve, g_x1b, p + 1)
                wait(dve, s_scat[slot], stored)
                for g in range(G):
                    a = dve.scalar_tensor_tensor(out=row[:, slot, g, 0:D], in0=ps_o[:, g], scalar=rix[:, g:g + 1],
                                                 in1=x1b[:, slot, g], op0=ALU.mult, op1=ALU.add)
                a.then_inc(d_x2, 1)

            def router_norm(p, slot):
                dve.wait_ge(d_x2, p + 1)
                norm_stats(p, 2, lambda g: row[:, slot, g, 0:D])

            def route(p, slot):
                wait(dve, pe_lg, p + 1)
                dve.tensor_tensor(lg[:, :, :], ps_lg,
                                  wrt[0:T, HALF * E:].rearrange("t (g e) -> t g e", g=G), ALU.add).then_inc(d_lg, 1)
                dve.wait_ge(d_lg, p + 1)
                dve.tensor_reduce(mxr[:, :, :], lg[:, :, :], AX.X, ALU.max).then_inc(d_mxr, 1)
                dve.wait_ge(d_mxr, p + 1)
                wait(dve, a_er, p)
                dve.tensor_tensor(dif[:, :, :], lg[:, :, :], mxr[:, :, :].to_broadcast([T, G, E]), ALU.subtract
                                  ).then_inc(d_dif, 1)
                dve.wait_ge(d_dif, p + 1)
                dve.tensor_scalar(key[:, :, :], dif[:, :, :], 0.0, float(E), ALU.is_lt, ALU.mult).then_inc(d_key, 1)
                dve.wait_ge(d_key, p + 1)
                dve.tensor_tensor(key2[:, :, :], key[:, :, :], iota, ALU.add).then_inc(d_key2, 1)
                dve.wait_ge(d_key2, p + 1)
                dve.tensor_reduce(idx[:, :, :], key2[:, :, :], AX.X, ALU.min).then_inc(d_idx, 1)
                dve.wait_ge(d_idx, p + 1)
                wait(dve, pe_rank, p)
                dve.tensor_tensor(oh[:, :, :], iota, idx[:, :, :].to_broadcast([T, G, E]), ALU.is_equal
                                  ).then_inc(d_oh, 1)

            def route_rows(p, slot, stored):
                wait(dve, a_er, p + 1)
                dve.tensor_reduce(sr[:, :], er[:, :, :], AX.X, ALU.add).then_inc(d_sr, 1)
                dve.wait_ge(d_sr, p + 1)
                dve.reciprocal(row[:, slot, :, C_PROB], sr[:, :]).then_inc(d_w, 1)
                wait(dve, pe_rank, p + 1)
                dve.wait_ge(d_oh, p + 1)
                dve.wait_ge(d_base, p + 1)
                for g in range(G):
                    a = dve.tensor_tensor(rk[:, g], ps_rk[:, g], base[:, slot], ALU.add)
                dve.tensor_tensor(base[:, 1 - slot], ps_tot, base[:, slot], ALU.add).then_inc(d_base, 1)
                dve.wait_ge(d_base, p + 2)
                dve.tensor_tensor(rk2[:, :, :], rk[:, :, :], oh[:, :, :], ALU.mult).then_inc(d_rk2, 1)
                dve.wait_ge(d_rk2, p + 1)
                dve.tensor_reduce(posf[:, :], rk2[:, :, :], AX.X, ALU.add).then_inc(d_posf, 1)
                dve.wait_ge(d_posf, p + 1)
                wait(dve, s_scat[slot], stored)
                dve.tensor_copy(pos[:, slot], posf[:, :]).then_inc(d_pos, 1)

            def own_constants():
                dve.wait_ge(l_cst, 16)
                dve.tensor_copy(up[:, :], cst[0:T, K_UP:K_UP + T])
                dve.memset(ones[:, :], 1.0)
                dve.memset(xp[:, :, S:], 0.0)
                dve.tensor_copy(base[:, 0], cst[0:T, K_EXP:K_EXP + E]).then_inc(d_base, 1)

            def step(s, k, half):
                if live(s + 2):
                    first_norm(s + 2, k, half * 16 + 32)
                if isinstance(s, int) and s == -2:
                    own_constants()
                if live(s + 1):
                    first_max(s + 1)
                if live(s - 1):
                    cross_residual(s - 1, 1 - k, 16 + (half - 1 + k) * 16 * G)
                    router_norm(s - 1, 1 - k)
                if live(s + 1):
                    first_sum(s + 1)
                if live(s):
                    cross_max(s, 0)
                if live(s - 2):
                    route_rows(s - 2, k, 16 + (half - 1) * 16 * G)
                if live(s):
                    cross_max(s, 1)
                if live(s + 1):
                    first_residual(s + 1, 1 - k)
                if live(s):
                    cross_sum(s)
                if live(s + 2):
                    rotate(s + 2)
                if live(s - 1):
                    if isinstance(s, int) and s == 1:
                        dve.wait_ge(l_router, 16)
                    route(s - 1, 1 - k)
                if isinstance(s, int) and s == -2:
                    dve.wait_ge(a_fold, 3)
                    dve.tensor_tensor(bvo[:, :], bank[5][0:T, D:2 * D], bfold[0:T, HALF + HALF * T:], ALU.add
                                      ).then_inc(d_bvo, 1)

            steps(dve, step)

            last = NP % 2
            n = 0

            def told(a):
                nonlocal n
                n += 1
                a.then_inc(d_bvo, 1)
                dve.wait_ge(d_bvo, n + 1)

            dve.wait_ge(d_base, NP + 1)
            told(dve.tensor_tensor(cnt[:, :], base[0:1, last], cst[0:1, K_EXP:K_EXP + E], ALU.subtract))
            c0 = cst[0:1, K_TILE:K_TILE + NTOK // P].rearrange("o (a n) -> o a n", a=1)
            told(dve.tensor_scalar(off1[0:1, 0:NTOK // P], cst[0:1, K_TILE:K_TILE + NTOK // P], float(P), None, ALU.mult))
            told(dve.tensor_tensor(big[:, :, :], cnt[:, :].rearrange("o (e a) -> o e a", a=1).to_broadcast([1, E, NTOK // P]),
                                   off1[0:1, 0:NTOK // P].rearrange("o (a n) -> o a n", a=1).to_broadcast([1, E, NTOK // P]),
                                   ALU.is_gt))
            told(dve.tensor_reduce(til[:, :], big[:, :, :], AX.X, ALU.add))
            told(dve.tensor_tensor_scan(cum[:, :], cst[0:1, K_ID:K_ID + 1].to_broadcast([1, E]), til[:, :], 0.0,
                                        ALU.mult, ALU.add))
            told(dve.tensor_tensor(ge[:, :, :],
                                   cst[0:1, K_TILE:K_TILE + TILES].rearrange("o (n a) -> o n a", a=1).to_broadcast([1, TILES, E]),
                                   cum[:, :].rearrange("o (a e) -> o a e", a=1).to_broadcast([1, TILES, E]), ALU.is_ge))
            told(dve.tensor_reduce(ex[:, :], ge[:, :, :], AX.X, ALU.add))
            told(dve.tensor_tensor(gt[:, :, :], ge[:, :, :],
                                   til[:, :].rearrange("o (a e) -> o a e", a=1).to_broadcast([1, TILES, E]), ALU.mult))
            told(dve.tensor_reduce(beg[:, :], gt[:, :, :], AX.X, ALU.add))
            told(dve.tensor_tensor(off1[:, :], cst[0:1, K_TILE:K_TILE + TILES], beg[:, :], ALU.subtract))
            told(dve.tensor_scalar(off2[:, :], off1[:, :], float(P), None, ALU.mult))
            told(dve.tensor_scalar(exc[:, :], ex[:, :], float(E - 1), None, ALU.min))
            dve.tensor_copy(tab_pad[:, :], base[0:1, last]).then_inc(d_tab, 1)
            dve.scalar_tensor_tensor(out=tab_row[:, :], in0=ex[:, :], scalar=float(CAP), in1=off2[:, :],
                                     op0=ALU.mult, op1=ALU.add).then_inc(d_tab, 1)
            dve.tensor_scalar(tab_w[:, :], exc[:, :], float(HALF * D), None, ALU.mult).then_inc(d_tab, 1)
            dve.tensor_scalar(tab_b[:, :], exc[:, :], float(D), None, ALU.mult).then_inc(d_tab, 1)
            dve.wait_ge(d_tab, 4)
            dve.wait_ge(l_bexp, 16)

            def tile(turn, k, rows):
                dve.wait_ge(l_rows[k], rows)
                wait(dve, s_out[k], rows - 16)
                dve.tensor_copy(eid[:, k:k + 1], er_ids[:, k, C_ID:C_ID + 1])
                wait(dve, pe_ey, turn * RING + k + 1)
                b = dve.value_load(tab_b[0:1, bass.ds(turn * RING + k, 1)], min_val=0, max_val=(E - 1) * D)
                dve.tensor_tensor(ey[:, k], bank[k][:, D:2 * D], bexp[:, bass.ds(b, D)], ALU.add).then_inc(d_ey, 1)
                dve.wait_ge(d_ey, turn * RING + k + 1)
                dve.scalar_tensor_tensor(out=eo[:, k], in0=ey[:, k], scalar=er_rows[:, k, C_PROB:C_PROB + 1],
                                         in1=er_rows[:, k, 0:D], op0=ALU.mult, op1=ALU.add).then_inc(d_eo, 1)

            for k in range(RING):
                tile(0, k, 16)
            with dve.Fori(1, TILES // RING) as i:
                for k in range(RING):
                    tile(i, k, i * 16 + 16)

        @block.gpsimd
        def _(pool):
            pool.memset(padt[:, :], 0.0).then_inc(g_const, 1)
            pool.wait_ge(g_const, 1)
            pool.memset(padt[:, C_ID:C_ID + 1].bitcast(I32), NO_TOKEN).then_inc(g_const, 1)
            pool.memset(mhalf[:, :], -0.5)
            pool.memset(step_ids[:, :], GT)
            pool.iota(row_int[:, 1, :, C_ID], pattern=[[T, G]], base=-GT, channel_multiplier=1).then_inc(g_id, 1)
            pool.wait_ge(g_id, 1)

            def powers(p, n, slot):
                wait(pool, d_ve[n], p + 1)
                used = (a_h1, a_h2, a_h3)[n]
                wait(pool, used, p - 1)
                pool.tensor_tensor(rs[n, slot][:, :], ve[n][:, :], mhalf[0:T, :], ALU.pow).then_inc(g_pow[n], 1)
                pool.wait_ge(g_pow[n], p + 1)
                pool.tensor_tensor(nm[n, slot][:, :], rs[n, slot][:, :], nmean[n][:, :], ALU.mult
                                   ).then_inc(g_rs[n], 1)

            def rotated(p):
                for t, dst, ready, done in ((tq, qr, d_tq, g_q), (tk, kr, d_tk, g_k)):
                    wait(pool, ready, p + 1)
                    wait(pool, pe_s, p)
                    for c in range(HALF):
                        a = pool.tensor_tensor(dst[:, c].rearrange("p g t -> p (g t)"), t[:, 0, c], t[:, 1, 1 - c],
                                               ALU.add)
                    a.then_inc(done, 1)

            def with_bias(p, slot):
                wait(pool, d_x1, p + 1)
                wait(pool, d_x2, p - 1)
                for g in range(G):
                    a = pool.tensor_tensor(x1b[:, slot, g], x1[:, slot, g], bvo[:, :], ALU.add)
                a.then_inc(g_x1b, 1)

            def scatter(p, slot, stored):
                wait(pool, s_scat[slot], stored)
                pool.wait_ge(g_id, p + 1)
                pool.wait_ge(g_rs[2], p + 1)
                pool.tensor_tensor(row_int[:, slot, :, C_ID], row_int[:, 1 - slot, :, C_ID], step_ids[:, :], ALU.add
                                   ).then_inc(g_id, 1)
                pool.wait_ge(g_id, p + 2)
                pool.wait_ge(d_w, p + 1)
                pool.wait_ge(d_pos, p + 1)
                pool.sem_inc(g_gate)
                for g in range(G):
                    pool.indirect_dma_start(
                        out=scratch, out_offset=bass.IndirectOffsetOnAxis(ap=pos[:, slot, g:g + 1].bitcast(U32), axis=0),
                        in_=row[:, slot, g, :], in_offset=None, bounds_check=SCR - 1, oob_is_err=False,
                    ).then_inc(s_scat[slot], 16)

            def idle_rows(slot):
                pool.wait_ge(g_const, 2)
                first, n = (0, IDLE // 2) if slot == 0 else (IDLE // 2, IDLE - IDLE // 2)
                pool.dma_start(scratch[E * CAP + first * P:E * CAP + (first + n) * P, :].rearrange("(n p) c -> p n c", p=P),
                             padt[:, :].rearrange("p (a c) -> p a c", a=1).to_broadcast([P, n, ROW])
                             ).then_inc(s_scat[slot], 16)

            def step(s, k, half):
                if live(s + 2):
                    powers(s + 2, 0, k)
                if live(s - 1):
                    powers(s - 1, 2, 1 - k)
                if live(s - 2):
                    scatter(s - 2, k, 16 + (half - 1) * 16 * G)
                if live(s + 1):
                    powers(s + 1, 1, 1 - k)
                if live(s + 2):
                    rotated(s + 2)
                if live(s + 1):
                    if isinstance(s, int) and s == -1:
                        pool.wait_ge(d_bvo, 1)
                    with_bias(s + 1, 1 - k)
                if isinstance(s, int) and s == -1:
                    idle_rows(0)
                    idle_rows(1)

            steps(pool, step)

            def tile(turn, k, rows):
                pool.wait_ge(d_eo, turn * RING + k + 1)
                pool.sem_inc(g_gate)
                pool.indirect_dma_start(
                    out=out_rows, out_offset=bass.IndirectOffsetOnAxis(ap=eid[:, k:k + 1], axis=0),
                    in_=eo[:, k], in_offset=None, bounds_check=NTOK - 1, oob_is_err=False,
                ).then_inc(s_out[k], 16)

            for k in range(RING):
                tile(0, k, 16)
            with pool.Fori(1, TILES // RING) as i:
                for k in range(RING):
                    tile(i, k, i * 16 + 16)


def constants():
    c = np.zeros((P, K_END), np.float32)
    c[:, K_ID:K_ID + P] = np.eye(P)
    half = D // 2
    inv = (1.0 / np.float32(10000.0) ** (np.arange(half, dtype=np.float32) / np.float32(half))).astype(np.float32)
    ang = (np.arange(T, dtype=np.float32)[None, :] * inv[:, None]).astype(np.float32)
    cos, sin = np.cos(ang).astype(np.float32), np.sin(ang).astype(np.float32)
    c[:, K_COS:K_COS + HALF * GT] = np.tile(cos, (1, HALF * G))
    c[:, K_SIN:K_SIN + GT] = np.tile(sin, (1, G))
    c[:, K_SIN + GT:K_SIN + 2 * GT] = np.tile(-sin, (1, G))
    t = np.arange(T)
    c[0:T, K_MASK:K_MASK + T] = np.where(t[None, :] <= t[:, None], 0.0, NEG)
    c[0:T, K_UP:K_UP + T] = t[:, None] < t[None, :]
    c[:, K_IOTA:K_IOTA + G * E] = np.tile(np.arange(E), G)
    c[:, K_EXP:K_EXP + E] = np.arange(E) * CAP
    c[:, K_TILE:K_TILE + TILES] = np.arange(TILES)
    return c


def by_halves(w):
    return np.ascontiguousarray(w.reshape(HALF, P, -1).transpose(1, 0, 2).reshape(P, -1))


def head_blocks(w):
    n = D // H
    full = np.zeros((HALF, n, H // HALF, n, H // HALF), w.dtype)
    for h in range(H):
        full[h % HALF, :, h // HALF, :, h // HALF] = w[:, :, h]
    return full.reshape(HALF, P, P).transpose(1, 0, 2).reshape(P, HALF * P)


def kernel(**inputs):
    import concourse.bacc as bacc
    from concourse.bass_utils import run_bass_kernel_spmd

    a = {n: np.asarray(v) for n, v in inputs.items()}
    ctx = a["ctx_1024"]
    nat = np.zeros((B, ST * P, D), ctx.dtype)
    nat[:, :S] = ctx
    nat = nat.reshape(B, ST, P, D).transpose(0, 2, 1, 3).reshape(B, P, NAT)
    trn = ctx.transpose(0, 2, 1).reshape(B, HALF, P, S).transpose(0, 2, 1, 3).reshape(B, P, TRN)
    both = np.concatenate([nat, trn], axis=2).reshape(NP, G, P, CW).transpose(0, 2, 1, 3).reshape(NP * P, G * CW)
    w_fold = np.concatenate([by_halves(a["L0_xattn_Wq"]), by_halves(a["L0_xattn_Wk"]), by_halves(a["L0_xattn_Wv"]),
                             by_halves(a["L0_xattn_Wo"].T)], axis=1)
    bv = np.repeat(a["L0_xattn_bv"].reshape(HALF, P).T, T, axis=1)
    b_fold = np.concatenate([a["L0_xattn_bq"].reshape(HALF, P).T, bv, np.tile(a["L0_xattn_bo"], (P, 1))], axis=1)
    w_router = np.concatenate([by_halves(a["L0_ffn_router_w"].T), np.tile(a["L0_ffn_router_b"], (P, G))], axis=1)
    w_expert = a["L0_ffn_expert_w"].transpose(0, 2, 1).reshape(E, HALF, P, D).transpose(2, 0, 1, 3).reshape(P, -1)
    arrays = {
        "x": a["x"], "ctxs": both, "consts": constants(),
        "w_self": np.concatenate([head_blocks(a[f"L0_attn_w_{n}"]) for n in "qkv"], axis=1),
        "w_fold": w_fold, "b_fold": b_fold, "w_router": w_router, "w_expert": w_expert,
        "b_expert": np.tile(a["L0_ffn_expert_b"].reshape(1, -1), (P, 1)),
    }
    arrays = {f"in_{n}": np.ascontiguousarray(v) for n, v in arrays.items()}
    nc = bacc.Bacc("TRN2", target_bir_lowering=False, num_devices=1)
    args = [nc.dram_tensor(n, v.shape, mybir.dt.from_np(v.dtype), kind="ExternalInput").ap()
            for n, v in arrays.items()]
    out = nc.dram_tensor("out", (B, T, D), F32, kind="ExternalOutput").ap()
    build(nc, *args, out)
    return run_bass_kernel_spmd(nc, [arrays], core_ids=[0]).results[0]["out"]
```

```python
from contextlib import ExitStack

import numpy as np

import concourse.bass as bass
from concourse import mybir

F32 = mybir.dt.float32
F32R = mybir.dt.float32r
BF16 = mybir.dt.bfloat16
I32 = mybir.dt.int32
U32 = mybir.dt.uint32
ALU = mybir.AluOpType
ACT = mybir.ActivationFunctionType
AX = mybir.AxisListType

B, T, D = 32, 112, 256
S = 375
H = 16
E = 8
P = 128
G = 2
NP = B // G
GT = G * T
HALF = D // P
ST = -(-S // P)
NAT = ST * D
TRN = HALF * S
CW = NAT + TRN
SCALE = float(D) ** -0.5
assert float(np.log2(SCALE)).is_integer()
EPS = 1e-5
BIG = 1e30

C_RSTD, C_SHIFT, C_PROB, C_ID, ROW = D, D + 1, D + 2, D + 3, D + 4
NTOK = B * T
CAP = P + NTOK
SCR = E * CAP
NO_TOKEN = 1 << 20
RING = 7
EARLY, EARLY_TURNS, TURNS = NP - 3, 2, 5
EARLY_TILES = EARLY_TURNS * RING
assert (EARLY + 1) * GT - E * (P - 1) > (EARLY_TILES - 1) * P
assert NTOK - EARLY_TILES * P + E * (P - 1) < ((TURNS - EARLY_TURNS) * RING + 1) * P
AHEAD = 2
FULL = NTOK // P
TW = 8
TT = TURNS * TW

K_ID, K_COS, K_SIN, K_MASK, K_UP, K_FALL, K_EXP, K_TILE, K_TROW, K_FULL, K_END = np.cumsum(
    [0, P, HALF * GT, HALF * GT, T, T, G * E, E, TT, TT, E * FULL]).tolist()


def wait(eng, sem, n):
    if isinstance(n, int) and n <= 0:
        return
    eng.wait_ge(sem, n)


def build(nc, x, ctxs, consts, w_self, w_fold, b_fold, w_router, w_expert, b_expert, out):
    with ExitStack() as stack:
        def sb(name, shape, dt=F32):
            return stack.enter_context(nc.sbuf_tensor(name, shape, dt))

        def split(name, shape):
            return [sb(f"{name}_{part}", shape, F32R) for part in ("high", "low")]

        def sem(name):
            return stack.enter_context(nc.semaphore(name))

        scratch = nc.dram_tensor("routed_rows", (SCR, ROW), F32).ap()
        x_rows = x.rearrange("b t d -> (b t) d")
        out_rows = out.rearrange("b t d -> (b t) d")

        cst = sb("cst", [P, K_END])
        ident = cst[:, K_ID:K_ID + P]
        cos2 = cst[:, K_COS:K_COS + HALF * GT]
        sin2 = cst[:, K_SIN:K_SIN + HALF * GT]
        causal = cst[0:T, K_MASK:K_MASK + T]
        falling = cst[0:T, K_FALL:K_FALL + G * E].rearrange("t (g e) -> t g e", g=G)
        up = sb("up", [T, T], BF16)
        ones = sb("ones", [T, T], BF16)
        wself = sb("wself", [P, 3, HALF, P])
        wqk_self = split("wqk_self", [P, 2, HALF, P])
        wfold = sb("wfold", [P, 4, HALF, D])
        bfold = sb("bfold", [P, HALF + HALF * T + D])
        wqk = split("wqk", [P, HALF, D])
        wvo = split("wvo", [P, HALF, D])
        bqk = sb("bqk", [P, HALF])
        bvo = sb("bvo", [T, D])
        wrt = sb("wrt", [P, HALF * E + G * E])
        wexp = sb("wexp", [P, E * HALF * D])
        bexp = sb("bexp", [P, E * D])
        mhalf = sb("mhalf", [P, G])
        padt = sb("padt", [P, ROW])
        step_ids = sb("step_ids", [T, G], I32)

        xs = sb("xs", [T, 2, G, D])
        h1 = sb("h1", [T, G, D])
        h1T = split("h1T", [P, HALF, G, T])
        h1T_sum = sb("h1T_sum", [P, HALF, G, T])
        tq = sb("tq", [P, 2, HALF, GT])
        tk = sb("tk", [P, 2, HALF, GT])
        qr = sb("qr", [P, HALF, G, T])
        kr = sb("kr", [P, HALF, G, T])
        v = sb("v", [T, G, D])
        sm = sb("sm", [T, G, T])
        p1 = sb("p1", [T, G, T])
        p1T = sb("p1T", [T, G, T])
        mn1 = sb("mn1", [T, G])
        sum1 = sb("sum1", [T, G])
        ri1 = sb("ri1", [T, G])
        cx = sb("cx", [P, 2, G, CW])
        x1 = sb("x1", [T, 2, G, D])
        x1b = sb("x1b", [T, 2, G, D])
        h2 = sb("h2", [T, G, D])
        h2T = split("h2T", [P, HALF, G, T])
        qt = sb("qt", [P, HALF, G, T])
        xp = sb("xp", [T, G, ST * P])
        xpT = sb("xpT", [P, G, ST, T])
        zT = split("zT", [P, HALF, G, T])
        mnx = sb("mnx", [T, G])
        sumx = sb("sumx", [T, G])
        rix = sb("rix", [T, G])
        row = sb("row", [T, 2, G, ROW])
        row_int = row[:, :, :, :].bitcast(I32)
        h3 = sb("h3", [T, G, D])
        h3T = sb("h3T", [P, HALF, G, T])
        lg = sb("lg", [T, G, E])
        mxr = sb("mxr", [T, G, 1])
        dif = sb("dif", [T, G, E])
        er = sb("er", [T, G, E])
        sr = sb("sr", [T, G])
        key = sb("key", [T, G, E])
        idx = sb("idx", [T, G, 1])
        oh = sb("oh", [T, G, E], BF16)
        rk = sb("rk", [T, G, E])
        rk2 = sb("rk2", [T, G, E])
        base = sb("base", [T, 2, E])
        posf = sb("posf", [T, G])
        pos = sb("pos", [T, 2, G], I32)
        st = [sb(f"st{n}", [T, G, 6]) for n in range(3)]
        mv = [sb(f"mv{n}", [T, G, 2]) for n in range(3)]
        ve = [sb(f"ve{n}", [T, G]) for n in range(3)]
        nmean = [sb(f"nmean{n}", [T, G]) for n in range(3)]
        rs = {(n, k): sb(f"rs{n}{k}", [T, G]) for n in range(2) for k in range(2)}
        nm = {(n, k): sb(f"nm{n}{k}", [T, G]) for n in range(2) for k in range(2)}
        for k in range(2):
            rs[2, k], nm[2, k] = row[:, k, :, C_RSTD], row[:, k, :, C_SHIFT]
        big = sb("big", [1, E, FULL])
        til = sb("til", [1, E])
        left = sb("left", [1, E])
        cum = sb("cum", [1, 2, E])
        w0 = sb("w0", [1, E])
        w = sb("w", [1, 2, E])
        dw = sb("dw", [1, 2, E])
        passed = sb("passed", [1, E + 1])
        early = sb("early", [1, E])
        ge = sb("ge", [1, TT, E])
        gt = sb("gt", [1, TT, E])
        ex = sb("ex", [1, TT])
        beg = sb("beg", [1, TT])
        off = sb("off", [1, TT])
        exc = sb("exc", [1, TT])
        tab_row = sb("tab_row", [1, TT], I32)
        tab_w = sb("tab_w", [1, TT], I32)
        tab_b = sb("tab_b", [1, TT], I32)
        er_rows = sb("er_rows", [P, RING, ROW])
        er_ids = er_rows[:, :, :].bitcast(U32)
        eid = sb("eid", [P, RING], U32)
        eh = sb("eh", [P, RING, D])
        ehT = sb("ehT", [P, RING, HALF, P])
        ey = sb("ey", [P, RING, D])
        eo = sb("eo", [P, RING, D])

        bank = [stack.enter_context(nc.psum_tensor(f"bank{n}", [P, 512], F32)) for n in range(8)]
        ps_T = bank[0][:, 0:HALF * GT].rearrange("p (c g t) -> p c g t", c=HALF, g=G)
        ps_q = bank[1][:, 0:HALF * GT].rearrange("p (c n) -> p c n", c=HALF)
        ps_k = bank[2][:, 0:HALF * GT].rearrange("p (c n) -> p c n", c=HALF)
        ps_v = bank[3][0:T, :].rearrange("t (g d) -> t g d", g=G)
        ps_y = ps_v
        ps_s = bank[4][0:T, 0:GT].rearrange("t (g k) -> t g k", g=G)
        ps_pT = bank[4][0:T, GT:2 * GT].rearrange("t (g k) -> t g k", g=G)
        ps_lg = bank[4][0:T, 2 * GT:2 * GT + G * E].rearrange("t (g e) -> t g e", g=G)
        ps_rk = bank[4][0:T, 2 * GT + G * E:2 * GT + 2 * G * E].rearrange("t (g e) -> t g e", g=G)
        ps_tot = bank[4][0:T, 2 * GT + 2 * G * E:2 * GT + 2 * G * E + E]
        ps_qt = [bank[n][:, 0:GT].rearrange("p (g t) -> p g t", g=G) for n in (5, 0)]
        ps_z = [bank[n][:, 0:GT].rearrange("p (g t) -> p g t", g=G) for n in (5, 7)]
        ps_xs = [bank[6 + g][0:T, 0:S] for g in range(G)]
        ps_xpT = [bank[6 + g][:, 0:ST * T].rearrange("p (n t) -> p n t", n=ST) for g in range(G)]
        ps_o = bank[6][0:T, :].rearrange("t (g d) -> t g d", g=G)

        TILE_BANKS = (1, 2, 3, 5, 6, 7, 3)
        ps_tile = [bank[n] for n in TILE_BANKS]

        l_ident, l_cst, l_self, l_fold, l_bfold, l_router, l_wexp, l_bexp = (
            sem(n) for n in ("l_ident", "l_cst", "l_self", "l_fold", "l_bfold", "l_router", "l_wexp", "l_bexp"))
        l_x = [sem(f"l_x{n}") for n in range(2)]
        l_cx = [sem(f"l_cx{n}") for n in range(2)]
        s_scat = [sem(f"s_scat{n}") for n in range(2)]
        l_rows = [sem(f"l_rows{n}") for n in range(RING)]
        s_out = [sem(f"s_out{n}") for n in range(RING)]
        (pe_h1T, pe_q, pe_k, pe_v, pe_s, pe_pT, pe_y, pe_h2T, pe_qt, pe_xs, pe_xpT, pe_z, pe_o, pe_h3T,
         pe_lg, pe_rank, pe_fold, pe_eT, pe_ey) = (sem(n) for n in (
            "pe_h1T pe_q pe_k pe_v pe_s pe_pT pe_y pe_h2T pe_qt pe_xs pe_xpT pe_z pe_o pe_h3T "
            "pe_lg pe_rank pe_fold pe_eT pe_ey").split())
        (a_self, a_h1, a_h1T, a_v, a_p1, a_pT, a_h2, a_h2T, a_qt, a_xp, a_xpT, a_z, a_h3, a_h3T, a_er, a_fold,
         a_eh, a_ehT) = (sem(n) for n in (
            "a_self a_h1 a_h1T a_v a_p1 a_pT a_h2 a_h2T a_qt a_xp a_xpT a_z a_h3 a_h3T a_er a_fold "
            "a_eh a_ehT").split())
        (d_self, d_fold, d_h1T, d_h2T, d_z, d_tq, d_tk, d_min1, d_ri1, d_x1, d_minx, d_rix, d_x2, d_lg, d_mxr, d_dif, d_w,
         d_key, d_idx, d_oh, d_rk2, d_posf, d_base, d_bvo, d_row, d_tab, d_ey, d_eo) = (sem(n) for n in (
            "d_self d_fold d_h1T d_h2T d_z d_tq d_tk d_min1 d_ri1 d_x1 d_minx d_rix d_x2 d_lg d_mxr d_dif d_w "
            "d_key d_idx d_oh d_rk2 d_posf d_base d_bvo d_row d_tab d_ey d_eo").split())
        d_st = [sem(f"d_st{n}") for n in range(3)]
        d_mv = [sem(f"d_mv{n}") for n in range(3)]
        g_const, g_h1T, g_q, g_k, g_x1b, g_id, g_pos = (
            sem(n) for n in "g_const g_h1T g_q g_k g_x1b g_id g_pos".split())
        d_gate, g_gate = sem("d_gate"), sem("g_gate")
        g_ve = [sem(f"g_ve{n}") for n in range(3)]
        g_pow = [sem(f"g_pow{n}") for n in range(3)]
        g_rs = [sem(f"g_rs{n}") for n in range(3)]

        def live(p):
            return not isinstance(p, int) or 0 <= p < NP

        def steps(eng, step):
            for s in range(-3, 2):
                step(s, s % 2, s // 2)
            with eng.Fori(1, NP // 2 - 2) as i:
                for k in range(2):
                    step(i * 2 + k, k, i)
            for s in range(NP - 4, NP + 2):
                step(s, s % 2, s // 2)

        def table(tab, turn, engine, most):
            return nc.values_load_multi_w_load_instructions(
                tab[0:1, bass.ds(turn * TW, RING)], engines=(engine,), min_val=0, max_val=most,
                skip_runtime_bounds_check_because="experts are clamped to E - 1, and a tile ends with its region at most")[1]

        block = stack.enter_context(nc.Block())

        @block.sync
        def _(sp):
            def load_x(p, slot):
                wait(sp, d_x1, p - 1)
                sp.dma_start(xs[:, slot], x_rows[bass.ds(p * GT, GT), :].rearrange("(g t) d -> t g d", g=G)
                             ).then_inc(l_x[slot], 16)

            def load_ctx(p, slot):
                wait(sp, pe_z, (p - 1) * HALF)
                sp.dma_start(cx[:, slot].rearrange("p g c -> p (g c)"), ctxs[bass.ds(p * P, P), :]
                             ).then_inc(l_cx[slot], 16)

            def step(s, k, half):
                if live(s + 1):
                    load_ctx(s + 1, 1 - k)
                if live(s + 3):
                    load_x(s + 3, 1 - k)
                if isinstance(s, int) and s == -3:
                    sp.dma_start(cst[:, 0:K_COS], consts[:, 0:K_COS]).then_inc(l_ident, 16)
                    sp.dma_start(cst[:, K_COS:], consts[:, K_COS:]).then_inc(l_cst, 16)
                if isinstance(s, int) and s == -2:
                    sp.dma_start(wfold[:, :, :, :].rearrange("p a c m -> p (a c m)"), w_fold).then_inc(l_fold, 16)
                    sp.dma_start(bfold[:, :], b_fold).then_inc(l_bfold, 16)
                if isinstance(s, int) and s == -1:
                    sp.dma_start(wrt[:, :], w_router).then_inc(l_router, 16)
                if isinstance(s, int) and s == 0:
                    sp.dma_start(wexp[:, :], w_expert).then_inc(l_wexp, 16)
                    sp.dma_start(bexp[:, :], b_expert).then_inc(l_bexp, 16)

            steps(sp, step)

            def turn_of_tiles(turn):
                rows = table(tab_row, turn, mybir.EngineType.SP, SCR - P)
                for k in range(RING):
                    wait(sp, d_eo, (turn - 1) * RING + k + 1)
                    sp.dma_start(er_rows[:, k, :], scratch[bass.ds(rows[k], P), :]).then_inc(l_rows[k], 16)

            sp.wait_ge(d_row, EARLY_TURNS)
            for n in range(2):
                sp.wait_ge(s_scat[n], 16 + 16 * G * (EARLY + 1) // 2)
            for turn in range(EARLY_TURNS):
                turn_of_tiles(turn)
            sp.wait_ge(d_row, TURNS)
            for n in range(2):
                sp.wait_ge(s_scat[n], 16 + 16 * G * NP // 2)
            with sp.Fori(EARLY_TURNS, TURNS) as i:
                turn_of_tiles(i)
            for k in range(RING):
                sp.wait_ge(s_out[k], 16 * TURNS)

        @block.tensor
        def _(pe):
            def first_transposes(p):
                wait(pe, a_h1, p + 1)
                wait(pe, a_qt, (p - 1) * HALF)
                for c in range(HALF):
                    for g in range(G):
                        m = pe.transpose(ps_T[:, c, g], h1[:, g, c::2], ident[0:T, 0:T])
                m.then_inc(pe_h1T, 1)

            def products(ps, pairs):
                for n, (a, b) in enumerate(pairs):
                    for i, (x, y) in enumerate(((0, 0), (0, 1), (1, 0))):
                        m = pe.matmul(ps, a[x], b[y], start=(n == 0 and i == 0), stop=(n == len(pairs) - 1 and i == 2))
                return m

            def first_product(p, n):
                ps, ready, used = ((ps_q, pe_q, d_tq), (ps_k, pe_k, d_tk))[n]
                wait(pe, d_h1T, p + 1)
                wait(pe, used, p)
                for c in range(HALF):
                    m = products(ps[:, c], [([w[:, n, c] for w in wqk_self],
                                             [h[:, c].rearrange("p g t -> p (g t)") for h in h1T])])
                m.then_inc(ready, 1)

            def first_v(p):
                wait(pe, d_x1, p)
                wait(pe, g_h1T, p + 1)
                for g in range(G):
                    for c in range(HALF):
                        m = pe.matmul(ps_v[:, g, c * P:(c + 1) * P], h1T_sum[:, c, g], wself[:, 2, c],
                                      start=True, stop=True)
                m.then_inc(pe_v, 1)

            def first_scores(p):
                wait(pe, g_q, p + 1)
                wait(pe, g_k, p + 1)
                wait(pe, d_min1, p * G)
                wait(pe, d_lg, p - 2)
                for g in range(G):
                    for c in range(HALF):
                        m = pe.matmul(ps_s[:, g], qr[:, c, g], kr[:, c, g], start=(c == 0), stop=(c == HALF - 1))
                m.then_inc(pe_s, 1)

            def first_probs_T(p):
                wait(pe, a_p1, (p + 1) * G)
                wait(pe, d_base, p - 1)
                for g in range(G):
                    m = pe.transpose(ps_pT[:, g], p1[:, g], ident[0:T, 0:T])
                m.then_inc(pe_pT, 1)

            def first_y(p):
                wait(pe, a_v, p + 1)
                wait(pe, a_pT, p + 1)
                for g in range(G):
                    m = pe.matmul(ps_y[:, g], p1T[:, g], v[:, g], start=True, stop=True)
                m.then_inc(pe_y, 1)

            def cross_transposes(p):
                wait(pe, a_h2, p + 1)
                wait(pe, a_h3T, p - 1)
                for c in range(HALF):
                    for g in range(G):
                        m = pe.transpose(ps_T[:, c, g], h2[:, g, c * P:(c + 1) * P], ident[0:T, 0:T])
                m.then_inc(pe_h2T, 1)

            def cross_queries(p):
                wait(pe, d_h2T, p + 1)
                wait(pe, d_z, p * HALF)
                for c in range(HALF):
                    products(ps_qt[c].rearrange("p g t -> p (g t)"),
                             [([w[:, n, c * P:(c + 1) * P] for w in wqk],
                               [h[:, n].rearrange("p g t -> p (g t)") for h in h2T]) for n in range(HALF)]
                             ).then_inc(pe_qt, 1)

            def cross_scores(p, slot, half, g):
                if g == 0:
                    pe.wait_ge(l_cx[slot], half * 16 + 16)
                    wait(pe, d_x2, p)
                wait(pe, a_xpT, (p - 1) * G + g + 1)
                for c in range(HALF):
                    if g == 0:
                        wait(pe, a_qt, p * HALF + c + 1)
                    m = pe.matmul(ps_xs[g], qt[:, c, g], cx[:, slot, g, NAT + c * S:NAT + (c + 1) * S],
                                  start=(c == 0), stop=(c == HALF - 1))
                m.then_inc(pe_xs, 1)

            def cross_probs_T(p, g):
                wait(pe, a_xp, p * G + g + 1)
                for n in range(ST):
                    m = pe.transpose(ps_xpT[g][:, n], xp[:, g, n * P:(n + 1) * P], ident[0:T, 0:T])
                m.then_inc(pe_xpT, 1)

            def cross_z(p, slot):
                for c in range(HALF):
                    for g in range(G):
                        if c == 0:
                            wait(pe, a_xpT, p * G + g + 1)
                        for n in range(ST):
                            m = pe.matmul(ps_z[c][:, g], cx[:, slot, g, n * D + c * P:n * D + (c + 1) * P],
                                          xpT[:, g, n], start=(n == 0), stop=(n == ST - 1))
                    m.then_inc(pe_z, 1)

            def cross_out(p):
                wait(pe, d_z, (p + 1) * HALF)
                for g in range(G):
                    m = products(ps_o[:, g], [([z[:, c, g] for z in zT], [w[:, c] for w in wvo]) for c in range(HALF)])
                m.then_inc(pe_o, 1)

            def router_transposes(p):
                wait(pe, a_h3, p + 1)
                if live(p + 3):
                    wait(pe, d_h1T, p + 4)
                else:
                    wait(pe, a_qt, min(p + 2, NP) * HALF)
                for c in range(HALF):
                    for g in range(G):
                        m = pe.transpose(ps_T[:, c, g], h3[:, g, c * P:(c + 1) * P], ident[0:T, 0:T])
                m.then_inc(pe_h3T, 1)

            def router_logits(p):
                wait(pe, a_h3T, p + 1)
                if live(p + 2):
                    wait(pe, a_pT, p + 3)
                else:
                    wait(pe, d_base, p + 1)
                for g in range(G):
                    for c in range(HALF):
                        m = pe.matmul(ps_lg[:, g], h3T[:, c, g], wrt[:, c * E:(c + 1) * E],
                                      start=(c == 0), stop=(c == HALF - 1))
                m.then_inc(pe_lg, 1)

            def ranks(p):
                wait(pe, d_oh, p + 1)
                pe.matmul(ps_rk[:, 0], up[:, :], oh[:, 0], start=True, stop=True)
                pe.matmul(ps_rk[:, 1], up[:, :], oh[:, 1], start=True, stop=False)
                pe.matmul(ps_rk[:, 1], ones[:, :], oh[:, 0], start=False, stop=True)
                pe.matmul(ps_tot, ones[:, :], oh[:, 0], start=True, stop=False)
                pe.matmul(ps_tot, ones[:, :], oh[:, 1], start=False, stop=True).then_inc(pe_rank, 1)

            def fold_weights(n):
                for c in range(HALF):
                    for e in range(HALF):
                        m = pe.matmul(bank[6 + n][:, c * D:(c + 1) * D], wfold[:, 2 * n, e, c * P:(c + 1) * P],
                                      wfold[:, 2 * n + 1, e, :], start=(e == 0), stop=(e == HALF - 1))
                m.then_inc(pe_fold, 1)

            def fold_biases():
                pe.wait_ge(l_bfold, 16)
                for c in range(HALF):
                    for e in range(HALF):
                        pe.matmul(bank[5][:, c:c + 1], wfold[:, 1, e, c * P:(c + 1) * P], bfold[:, e:e + 1],
                                  start=(e == 0), stop=(e == HALF - 1))
                for e in range(HALF):
                    m = pe.matmul(bank[5][0:T, D:2 * D], bfold[:, HALF + e * T:HALF + (e + 1) * T],
                                  wfold[:, 3, e, :], start=(e == 0), stop=(e == HALF - 1))
                m.then_inc(pe_fold, 1)

            def tile_T(turn, k):
                wait(pe, a_eh, turn * RING + k + 1)
                same = max(n for n in range(-RING, k) if TILE_BANKS[n % RING] == TILE_BANKS[k])
                wait(pe, d_ey, turn * RING + same + 1)
                for c in range(HALF):
                    m = pe.transpose(ps_tile[k][:, c * P:(c + 1) * P], eh[:, k, c * P:(c + 1) * P], ident)
                m.then_inc(pe_eT, 1)

            def tile(turn, k, starts, more=True):
                if more:
                    tile_T(turn + (k + 1) // RING, (k + 1) % RING)
                wait(pe, a_ehT, turn * RING + k + 1)
                for c in range(HALF):
                    m = pe.matmul(ps_tile[k][:, D:2 * D], ehT[:, k, c], wexp[:, bass.ds(starts[k] + c * D, D)],
                                  start=(c == 0), stop=(c == HALF - 1))
                m.then_inc(pe_ey, 1)

            def expert_weights(turn):
                wait(pe, d_tab, turn + 1)
                return table(tab_w, turn, mybir.EngineType.PE, (E - 1) * HALF * D)

            def turn_of_tiles(turn, last=False):
                starts = expert_weights(turn)
                for k in range(RING):
                    tile(turn, k, starts, more=not last or k + 1 < RING)

            starts = []

            pe.wait_ge(l_ident, 16)

            def step(s, k, half):
                if live(s + 1):
                    first_scores(s + 1)
                if live(s - 2):
                    ranks(s - 2)
                if isinstance(s, int) and s == NP:
                    pe.wait_ge(l_wexp, 16)
                    starts.extend(expert_weights(0))
                    tile_T(0, 0)
                    for n in range(3):
                        tile(0, n, starts)
                if isinstance(s, int) and s == NP + 1:
                    tile(0, 6, starts)
                if live(s):
                    if isinstance(s, int) and s == 0:
                        pe.wait_ge(d_fold, 2)
                        pe.wait_ge(a_fold, 3)
                        pe.wait_ge(d_bvo, 1)
                    cross_queries(s)
                if live(s + 1):
                    first_v(s + 1)
                if live(s):
                    cross_scores(s, k, half, 0)
                if live(s + 1):
                    first_probs_T(s + 1)
                if live(s + 2):
                    first_transposes(s + 2)
                if live(s):
                    cross_scores(s, k, half, 1)
                if live(s + 1):
                    first_y(s + 1)
                if live(s):
                    cross_probs_T(s, 0)
                if live(s + 2):
                    if isinstance(s, int) and s == -2:
                        pe.wait_ge(d_self, 1)
                    first_product(s + 2, 0)
                if live(s):
                    cross_probs_T(s, 1)
                if live(s + 2):
                    first_product(s + 2, 1)
                if live(s - 1):
                    router_transposes(s - 1)
                if live(s):
                    cross_z(s, k)
                if live(s - 1):
                    if isinstance(s, int) and s == 1:
                        pe.wait_ge(l_router, 16)
                    if isinstance(s, int) and s == NP:
                        tile(0, 3, starts)
                    router_logits(s - 1)
                    if isinstance(s, int) and s == NP:
                        tile(0, 4, starts)
                        tile(0, 5, starts)
                if isinstance(s, int) and s == -1:
                    fold_weights(1)
                    fold_biases()
                if live(s + 1):
                    cross_transposes(s + 1)
                if live(s):
                    cross_out(s)
                if isinstance(s, int) and s == -2:
                    pe.wait_ge(l_fold, 16)
                    fold_weights(0)

            steps(pe, step)

            with pe.Fori(1, TURNS - 1) as i:
                turn_of_tiles(i)
            turn_of_tiles(TURNS - 1, last=True)

        @block.scalar
        def _(act):
            act.dma_start(wself[:, :, :, :].rearrange("p a c m -> p (a c m)"), w_self).then_inc(l_self, 16)
            act.wait_ge(l_self, 16)
            act.activation(wqk_self[0][:, 0], wself[:, 0], ACT.Copy, scale=-SCALE)
            act.activation(wqk_self[0][:, 1], wself[:, 1], ACT.Copy).then_inc(a_self, 1)

            def norm(p, n, slot, dst, src, done, used):
                wait(act, g_rs[n], p + 1)
                wait(act, used, p)
                for g in range(G):
                    a = act.activation(dst[:, g], src(g), ACT.Identity, bias=nm[n, slot][:, g:g + 1],
                                       scale=rs[n, slot][:, g:g + 1])
                a.then_inc(done, 1)

            def evacuate(dst, src, ready, n_ready, used, n_used, done):
                wait(act, ready, n_ready)
                wait(act, used, n_used)
                act.activation(dst, src, ACT.Copy).then_inc(done, 1)

            def fold(n, dst, scale):
                act.wait_ge(pe_fold, n)
                act.activation(dst[0][:, :, :], bank[5 + n][:, :].rearrange("p (c d) -> p c d", c=HALF), ACT.Copy,
                               scale=scale).then_inc(a_fold, 1)

            def tile_norm(turn, k):
                act.wait_ge(l_rows[k], turn * 16 + 16)
                wait(act, pe_eT, (turn - 1) * RING + k + 1)
                act.activation(eh[:, k], er_rows[:, k, 0:D], ACT.Identity, bias=er_rows[:, k, C_SHIFT:C_SHIFT + 1],
                               scale=er_rows[:, k, C_RSTD:C_RSTD + 1]).then_inc(a_eh, 1)

            def tile(turn, k, more=True):
                if more:
                    tile_norm(turn + (k + AHEAD) // RING, (k + AHEAD) % RING)
                wait(act, pe_eT, turn * RING + k + 1)
                wait(act, pe_ey, (turn - 1) * RING + k + 1)
                act.activation(ehT[:, k], ps_tile[k][:, 0:D].rearrange("p (c t) -> p c t", c=HALF), ACT.Copy
                               ).then_inc(a_ehT, 1)

            def turn_of_tiles(turn, last=False):
                for k in range(RING):
                    tile(turn, k, more=not last or k + AHEAD < RING)

            def step(s, k, half):
                p = s + 2
                if live(p):
                    norm(p, 0, k, h1, lambda g: xs[:, k, g], a_h1, pe_h1T)
                p = s - 2
                if live(p):
                    wait(act, d_dif, p + 1)
                    wait(act, d_w, p)
                    for g in range(G):
                        act.activation(er[:, g], dif[:, g], ACT.Exp, accum_out=sr[:, g:g + 1]).then_inc(a_er, 1)
                if isinstance(s, int) and s == NP:
                    for n in range(AHEAD):
                        tile_norm(0, n)
                    for n in range(3):
                        tile(0, n)
                if isinstance(s, int) and s == NP + 1:
                    tile(0, 6)
                p = s
                if live(p):
                    for c in range(HALF):
                        wait(act, pe_qt, p * HALF + c + 1)
                        wait(act, pe_xs, p * G)
                        act.activation(qt[:, c], ps_qt[c], ACT.Identity, bias=bqk[:, c:c + 1]).then_inc(a_qt, 1)
                p = s + 1
                if live(p):
                    wait(act, d_min1, (p + 1) * G)
                    wait(act, pe_pT, p)
                    wait(act, d_ri1, p)
                    for g in range(G):
                        act.activation(p1[:, g], sm[:, g], ACT.Exp, bias=mn1[:, g:g + 1], scale=-1.0,
                                       accum_out=sum1[:, g:g + 1]).then_inc(a_p1, 1)
                    wait(act, pe_v, p + 1)
                    wait(act, pe_y, p)
                    for g in range(G):
                        a = act.activation(v[:, g].rearrange("t (i c) -> t c i", c=HALF),
                                           ps_v[:, g].rearrange("t (c i) -> t c i", c=HALF), ACT.Copy)
                    a.then_inc(a_v, 1)
                p = s + 1
                if live(p):
                    evacuate(p1T[:, :, :], ps_pT, pe_pT, p + 1, pe_y, p, a_pT)
                p = s + 2
                if live(p):
                    evacuate(h1T[0][:, :, :, :], ps_T, pe_h1T, p + 1, g_h1T, p, a_h1T)
                for g in range(G):
                    if live(s):
                        wait(act, d_minx, s * G + g + 1)
                        wait(act, pe_xpT, (s - 1) * G + g + 1)
                        if g == 0:
                            wait(act, d_rix, s)
                        act.activation(xp[:, g, 0:S], ps_xs[g], ACT.Exp, bias=mnx[:, g:g + 1], scale=-1.0,
                                       accum_out=sumx[:, g:g + 1]).then_inc(a_xp, 1)
                    p = s - 1
                    if g == 0 and live(p):
                        norm(p, 2, 1 - k, h3, lambda g: row[:, 1 - k, g, 0:D], a_h3, pe_h3T)
                p = s
                if live(p):
                    for g in range(G):
                        evacuate(xpT[:, g], ps_xpT[g], pe_xpT, p * G + g + 1, pe_z, p * HALF, a_xpT)
                if isinstance(s, int) and s == NP:
                    tile(0, 3)
                p = s - 1
                if live(p):
                    evacuate(h3T[:, :, :, :], ps_T, pe_h3T, p + 1, pe_lg, p, a_h3T)
                p = s + 1
                if live(p):
                    norm(p, 1, 1 - k, h2, lambda g: x1[:, 1 - k, g], a_h2, pe_h2T)
                p = s
                if live(p):
                    for c in range(HALF):
                        evacuate(zT[0][:, c], ps_z[c], pe_z, p * HALF + c + 1, pe_o, p, a_z)
                if isinstance(s, int) and s == -1:
                    fold(2, wvo, 1.0)
                    act.wait_ge(pe_fold, 3)
                    act.activation(bqk[:, :], bank[5][:, 0:HALF], ACT.Copy, scale=-SCALE).then_inc(a_fold, 1)
                p = s + 1
                if live(p):
                    evacuate(h2T[0][:, :, :, :], ps_T, pe_h2T, p + 1, pe_qt, p * HALF, a_h2T)
                if isinstance(s, int) and s == -2:
                    fold(1, wqk, -SCALE)
                if isinstance(s, int) and s == NP:
                    tile(0, 4)
                    tile(0, 5)

            steps(act, step)

            with act.Fori(1, TURNS - 1) as i:
                turn_of_tiles(i)
            turn_of_tiles(TURNS - 1, last=True)

        @block.vector
        def _(dve):
            def norm_sums(p, n, src):
                for g in range(G):
                    a = dve.bn_stats(st[n][:, g], src(g))
                a.then_inc(d_st[n], 1)

            def norm_means(p, n):
                dve.wait_ge(d_st[n], p + 1)
                wait(dve, g_ve[n], p)
                dve.sem_inc(d_gate)
                for g in range(G):
                    a = dve.bn_aggr(mv[n][:, g], st[n][:, g])
                a.then_inc(d_mv[n], 1)

            def first_norm(p, slot, n):
                dve.wait_ge(l_x[slot], n)
                norm_sums(p, 0, lambda g: xs[:, slot, g])

            def low_part(low, ps, high, p, evacuated, used, n_used, done):
                wait(dve, evacuated, p + 1)
                wait(dve, used, n_used)
                dve.tensor_tensor(low, ps, high.bitcast(F32), ALU.subtract).then_inc(done, 1)

            def fold(n, dst, scale):
                dve.wait_ge(a_fold, n)
                dve.scalar_tensor_tensor(out=dst[1][:, :, :], in0=bank[5 + n][:, :].rearrange("p (c d) -> p c d", c=HALF),
                                         scalar=scale, in1=dst[0][:, :, :].bitcast(F32), op0=ALU.mult,
                                         op1=ALU.subtract).then_inc(d_fold, 1)

            def rotate(p):
                for ps, t, ready, used, done in ((ps_q, tq, pe_q, g_q, d_tq), (ps_k, tk, pe_k, g_k, d_tk)):
                    wait(dve, ready, p + 1)
                    wait(dve, used, p)
                    dve.tensor_tensor(t[:, 0], ps, cos2.rearrange("p (c n) -> p c n", c=HALF), ALU.mult)
                    dve.tensor_tensor(t[:, 1], ps, sin2.rearrange("p (c n) -> p c n", c=HALF), ALU.mult
                                      ).then_inc(done, 1)

            def first_min(p):
                for g in range(G):
                    wait(dve, pe_s, p + 1)
                    wait(dve, pe_rank, p - 2)
                    wait(dve, a_p1, (p - 1) * G + g + 1)
                    dve.sem_inc(d_gate)
                    dve.tensor_tensor_reduce(out=sm[:, g], in0=ps_s[:, g], in1=causal, scale=1.0, scalar=3e38,
                                             op0=ALU.add, op1=ALU.min, accum_out=mn1[:, g:g + 1]
                                             ).then_inc(d_min1, 1)

            def first_sum(p):
                wait(dve, a_p1, (p + 1) * G)
                dve.reciprocal(ri1[:, :], sum1[:, :]).then_inc(d_ri1, 1)

            def first_residual(p, slot):
                dve.wait_ge(d_ri1, p + 1)
                wait(dve, pe_y, p + 1)
                wait(dve, g_x1b, p - 1)
                wait(dve, a_h2, p - 1)
                for g in range(G):
                    a = dve.scalar_tensor_tensor(out=x1[:, slot, g], in0=ps_y[:, g], scalar=ri1[:, g:g + 1],
                                                 in1=xs[:, slot, g], op0=ALU.mult, op1=ALU.add)
                a.then_inc(d_x1, 1)

            def cross_norm(p, slot):
                dve.wait_ge(d_x1, p + 1)
                norm_sums(p, 1, lambda g: x1[:, slot, g])

            def cross_min(p, g):
                wait(dve, pe_xs, p * G + g + 1)
                wait(dve, a_xp, (p - 1) * G + g + 1)
                dve.tensor_reduce(mnx[:, g:g + 1], ps_xs[g], AX.X, ALU.min).then_inc(d_minx, 1)

            def cross_sum(p):
                wait(dve, a_xp, (p + 1) * G)
                dve.reciprocal(rix[:, :], sumx[:, :]).then_inc(d_rix, 1)

            def cross_residual(p, slot, stored):
                dve.wait_ge(d_rix, p + 1)
                wait(dve, pe_o, p + 1)
                wait(dve, g_x1b, p + 1)
                wait(dve, s_scat[slot], stored)
                for g in range(G):
                    a = dve.scalar_tensor_tensor(out=row[:, slot, g, 0:D], in0=ps_o[:, g], scalar=rix[:, g:g + 1],
                                                 in1=x1b[:, slot, g], op0=ALU.mult, op1=ALU.add)
                a.then_inc(d_x2, 1)

            def router_norm(p, slot):
                dve.wait_ge(d_x2, p + 1)
                norm_sums(p, 2, lambda g: row[:, slot, g, 0:D])

            def router_bias(p):
                wait(dve, pe_lg, p + 1)
                dve.tensor_tensor(lg[:, :, :], ps_lg,
                                  wrt[0:T, HALF * E:].rearrange("t (g e) -> t g e", g=G), ALU.add).then_inc(d_lg, 1)

            def router_max(p):
                dve.wait_ge(d_lg, p + 1)
                dve.tensor_reduce(mxr[:, :, :], lg[:, :, :], AX.X, ALU.max).then_inc(d_mxr, 1)

            def route(p):
                dve.wait_ge(d_mxr, p + 1)
                wait(dve, a_er, p * G)
                dve.tensor_tensor(dif[:, :, :], lg[:, :, :], mxr[:, :, :].to_broadcast([T, G, E]), ALU.subtract
                                  ).then_inc(d_dif, 1)
                dve.wait_ge(d_dif, p + 1)
                dve.scalar_tensor_tensor(out=key[:, :, :], in0=dif[:, :, :], scalar=0.0, in1=falling,
                                         op0=ALU.is_ge, op1=ALU.mult).then_inc(d_key, 1)
                dve.wait_ge(d_key, p + 1)
                dve.tensor_reduce(idx[:, :, :], key[:, :, :], AX.X, ALU.max).then_inc(d_idx, 1)
                dve.wait_ge(d_idx, p + 1)
                wait(dve, pe_rank, p)
                dve.tensor_tensor(oh[:, :, :], falling, idx[:, :, :].to_broadcast([T, G, E]), ALU.is_equal
                                  ).then_inc(d_oh, 1)

            def route_rows(p, slot):
                wait(dve, pe_rank, p + 1)
                dve.wait_ge(d_base, p + 1)
                dve.tensor_tensor(rk[:, :, :], ps_rk, base[:, slot].rearrange("t (a e) -> t a e", a=1
                                                                             ).to_broadcast([T, G, E]), ALU.add)
                dve.tensor_tensor(base[:, 1 - slot], ps_tot, base[:, slot], ALU.add).then_inc(d_base, 1)
                wait(dve, a_er, (p + 1) * G)
                dve.reciprocal(row[:, slot, :, C_PROB], sr[:, :]).then_inc(d_w, 1)
                dve.wait_ge(d_base, p + 2)
                dve.tensor_tensor(rk2[:, :, :], rk[:, :, :], oh[:, :, :], ALU.mult).then_inc(d_rk2, 1)

            def route_row(p):
                dve.wait_ge(d_rk2, p + 1)
                wait(dve, g_pos, p)
                dve.tensor_reduce(posf[:, :], rk2[:, :, :], AX.X, ALU.add).then_inc(d_posf, 1)

            told_n = 0

            def told(a):
                nonlocal told_n
                told_n += 1
                a.then_inc(d_bvo, 1)
                dve.wait_ge(d_bvo, told_n + 1)

            full = cst[0:1, K_FULL:K_FULL + E * FULL].rearrange("o (e n) -> o e n", e=E)

            def over(v, n):
                return v.rearrange("o (a e) -> o a e", a=1).to_broadcast([1, n, E])

            def ends(v, n):
                return v.rearrange("o (e a) -> o e a", a=1).to_broadcast([1, E, n])

            def sum_over_experts(part, src):
                told(dve.tensor_tensor_scan(cum[:, part], cst[0:1, K_ID:K_ID + 1].to_broadcast([1, E]), src, 0.0,
                                            ALU.mult, ALU.add))

            def tile_tables(part):
                turns = (0, EARLY_TURNS) if part == 0 else (EARLY_TURNS, TURNS)
                these = slice(turns[0] * TW, turns[1] * TW)
                n = these.stop - these.start
                number = cst[0:1, K_TILE + these.start:K_TILE + these.stop].rearrange("o (n a) -> o n a", a=1)
                dve.tensor_tensor(dw[:, part, 0:E - 1], w[:, part, 1:E], w[:, part, 0:E - 1], ALU.subtract)
                told(dve.tensor_tensor(ge[:, these], number.to_broadcast([1, n, E]), over(cum[:, part], n), ALU.is_ge))
                told(dve.tensor_tensor(gt[:, these], ge[:, these], over(dw[:, part], n), ALU.mult))
                told(dve.tensor_reduce(beg[:, these], gt[:, these], AX.X, ALU.add))
                told(dve.tensor_tensor(off[:, these], beg[:, these], cst[0:1, K_TROW + these.start:K_TROW + these.stop],
                                       ALU.add))
                dve.tensor_scalar(tab_row[:, these], off[:, these], w[:, part, 0:1], 0.0, ALU.add, ALU.max
                                  ).then_inc(d_row, turns[1] - turns[0])
                told(dve.tensor_reduce(ex[:, these], ge[:, these], AX.X, ALU.add))
                told(dve.tensor_scalar(exc[:, these], ex[:, these], float(E - 1), None, ALU.min))
                dve.tensor_scalar(tab_w[:, these], exc[:, these], float(HALF * D), None, ALU.mult)
                dve.tensor_scalar(tab_b[:, these], exc[:, these], float(D), None, ALU.mult
                                  ).then_inc(d_tab, turns[1] - turns[0])

            def early_turns():
                after = base[0:1, (EARLY + 1) % 2]
                dve.wait_ge(d_base, EARLY + 2)
                told(dve.tensor_tensor(big[:, :, 1:], ends(after, FULL - 1), full[:, :, 1:], ALU.is_ge))
                told(dve.tensor_reduce(til[:, :], big[:, :, 1:], AX.X, ALU.add))
                sum_over_experts(0, til[:, :])
                told(dve.scalar_tensor_tensor(out=w0[:, :], in0=cum[:, 0], scalar=-float(P),
                                              in1=cst[0:1, K_EXP:K_EXP + E], op0=ALU.mult, op1=ALU.add))
                told(dve.scalar_tensor_tensor(out=w[:, 0], in0=til[:, :], scalar=float(P), in1=w0[:, :],
                                              op0=ALU.mult, op1=ALU.add))
                tile_tables(0)
                told(dve.tensor_scalar(passed[:, 1:], cum[:, 0], float(EARLY_TILES), None, ALU.min))
                told(dve.tensor_tensor(early[:, :], passed[:, 1:], passed[:, 0:E], ALU.subtract))

            def other_turns():
                after = base[0:1, NP % 2]
                dve.wait_ge(d_base, NP + 1)
                told(dve.tensor_tensor(big[:, :, :], ends(after, FULL), full, ALU.is_gt))
                told(dve.tensor_reduce(til[:, :], big[:, :, :], AX.X, ALU.add))
                told(dve.tensor_tensor(left[:, :], til[:, :], early[:, :], ALU.subtract))
                sum_over_experts(1, left[:, :])
                told(dve.scalar_tensor_tensor(out=w[:, 1], in0=cum[:, 1], scalar=-float(P), in1=after,
                                              op0=ALU.mult, op1=ALU.add))
                tile_tables(1)

            def tile(turn, k, rows, starts):
                dve.wait_ge(l_rows[k], rows)
                wait(dve, s_out[k], rows - 16)
                dve.tensor_copy(eid[:, k:k + 1], er_ids[:, k, C_ID:C_ID + 1])
                wait(dve, pe_ey, turn * RING + k + 1)
                dve.tensor_tensor(ey[:, k], ps_tile[k][:, D:2 * D], bexp[:, bass.ds(starts[k], D)], ALU.add
                                  ).then_inc(d_ey, 1)
                dve.wait_ge(d_ey, turn * RING + k + 1)
                dve.scalar_tensor_tensor(out=eo[:, k], in0=ey[:, k], scalar=er_rows[:, k, C_PROB:C_PROB + 1],
                                         in1=er_rows[:, k, 0:D], op0=ALU.mult, op1=ALU.add).then_inc(d_eo, 1)

            starts = []

            def own_constants():
                dve.wait_ge(l_cst, 16)
                dve.tensor_copy(up[:, :], cst[0:T, K_UP:K_UP + T])
                dve.memset(ones[:, :], 1.0)
                dve.memset(xp[:, :, S:], 0.0)
                dve.memset(dw[:, :, E - 1:E], -float(1 << 22))
                dve.memset(passed[:, 0:1], 0.0)
                dve.tensor_copy(base[:, 0], cst[0:T, K_EXP:K_EXP + E]).then_inc(d_base, 1)

            def step(s, k, half):
                if live(s - 1):
                    cross_residual(s - 1, 1 - k, 16 + (half - 1 + k) * 16 * G)
                if live(s + 1):
                    first_min(s + 1)
                if live(s - 1):
                    router_norm(s - 1, 1 - k)
                if live(s - 2):
                    route_rows(s - 2, k)
                if live(s - 1):
                    norm_means(s - 1, 2)
                if live(s - 2):
                    route_row(s - 2)
                if live(s + 1):
                    first_sum(s + 1)
                if live(s):
                    cross_min(s, 0)
                if live(s + 2):
                    low_part(h1T[1][:, :, :, :], ps_T, h1T[0][:, :, :, :], s + 2, a_h1T, g_h1T, s + 2, d_h1T)
                if live(s):
                    cross_min(s, 1)
                if live(s + 1):
                    first_residual(s + 1, 1 - k)
                if live(s):
                    cross_sum(s)
                if isinstance(s, int) and s == EARLY + 2:
                    early_turns()
                if live(s + 1):
                    cross_norm(s + 1, 1 - k)
                    norm_means(s + 1, 1)
                if live(s + 2):
                    rotate(s + 2)
                if live(s + 3):
                    first_norm(s + 3, 1 - k, (half + k) * 16 + 32)
                if live(s):
                    for c in range(HALF):
                        low_part(zT[1][:, c], ps_z[c], zT[0][:, c], s * HALF + c, a_z, pe_o, s, d_z)
                if isinstance(s, int) and s == NP:
                    dve.wait_ge(d_tab, EARLY_TURNS)
                    dve.wait_ge(l_bexp, 16)
                    starts.extend(table(tab_b, 0, mybir.EngineType.DVE, (E - 1) * D))
                    for n in range(4):
                        tile(0, n, 16, starts)
                if live(s - 1):
                    if isinstance(s, int) and s == 1:
                        dve.wait_ge(l_router, 16)
                    router_bias(s - 1)
                if live(s + 3):
                    norm_means(s + 3, 0)
                if live(s - 1):
                    router_max(s - 1)
                    route(s - 1)
                if isinstance(s, int) and s == -1:
                    fold(2, wvo, 1.0)
                    dve.wait_ge(a_fold, 3)
                    dve.tensor_tensor(bvo[:, :], bank[5][0:T, D:2 * D], bfold[0:T, HALF + HALF * T:], ALU.add
                                      ).then_inc(d_bvo, 1)
                if live(s + 1):
                    low_part(h2T[1][:, :, :, :], ps_T, h2T[0][:, :, :, :], s + 1, a_h2T, pe_qt, (s + 1) * HALF, d_h2T)
                if isinstance(s, int) and s == NP:
                    tile(0, 4, 16, starts)
                if isinstance(s, int) and s == -3:
                    own_constants()
                    dve.wait_ge(a_self, 1)
                    dve.scalar_tensor_tensor(out=wqk_self[1][:, 0], in0=wself[:, 0], scalar=-SCALE,
                                             in1=wqk_self[0][:, 0].bitcast(F32), op0=ALU.mult, op1=ALU.subtract)
                    dve.tensor_tensor(wqk_self[1][:, 1], wself[:, 1], wqk_self[0][:, 1].bitcast(F32), ALU.subtract
                                      ).then_inc(d_self, 1)
                if isinstance(s, int) and s == -2:
                    fold(1, wqk, -SCALE)

            steps(dve, step)
            other_turns()
            for n in range(5, RING):
                tile(0, n, 16, starts)
            dve.wait_ge(d_tab, TURNS)
            with dve.Fori(1, TURNS) as i:
                rest = table(tab_b, i, mybir.EngineType.DVE, (E - 1) * D)
                for k in range(RING):
                    tile(i, k, i * 16 + 16, rest)

        @block.gpsimd
        def _(pool):
            pool.memset(padt[:, :], 0.0).then_inc(g_const, 1)
            pool.wait_ge(g_const, 1)
            pool.memset(padt[:, C_ID:C_ID + 1].bitcast(I32), NO_TOKEN).then_inc(g_const, 1)
            pool.memset(mhalf[:, :], -0.5)
            pool.memset(step_ids[:, :], GT)
            pool.iota(row_int[:, 1, :, C_ID], pattern=[[T, G]], base=-GT, channel_multiplier=1).then_inc(g_id, 1)
            pool.wait_ge(g_id, 1)

            def powers(p, n, slot):
                wait(pool, d_mv[n], p + 1)
                if n < 2:
                    wait(pool, (a_h1, a_h2)[n], p - 1)
                pool.sem_inc(g_gate)
                pool.tensor_scalar(ve[n][:, :], mv[n][:, :, 1], EPS, None, ALU.add)
                pool.tensor_scalar(nmean[n][:, :], mv[n][:, :, 0], -1.0, None, ALU.mult).then_inc(g_ve[n], 1)
                pool.wait_ge(g_ve[n], p + 1)
                pool.tensor_tensor(rs[n, slot][:, :], ve[n][:, :], mhalf[0:T, :], ALU.pow).then_inc(g_pow[n], 1)
                pool.wait_ge(g_pow[n], p + 1)
                pool.tensor_tensor(nm[n, slot][:, :], rs[n, slot][:, :], nmean[n][:, :], ALU.mult
                                   ).then_inc(g_rs[n], 1)

            def rotated(p):
                for t, dst, ready, done in ((tq, qr, d_tq, g_q), (tk, kr, d_tk, g_k)):
                    wait(pool, ready, p + 1)
                    wait(pool, pe_s, p)
                    for c in range(HALF):
                        a = pool.tensor_tensor(dst[:, c].rearrange("p g t -> p (g t)"), t[:, 0, c], t[:, 1, 1 - c],
                                               ALU.add)
                    a.then_inc(done, 1)

            def with_bias(p, slot):
                wait(pool, d_x1, p + 1)
                wait(pool, d_x2, p - 1)
                for g in range(G):
                    a = pool.tensor_tensor(x1b[:, slot, g], x1[:, slot, g], bvo[:, :], ALU.add)
                a.then_inc(g_x1b, 1)

            def scatter(p, slot, stored):
                wait(pool, s_scat[slot], stored)
                pool.wait_ge(g_id, p + 1)
                pool.wait_ge(g_rs[2], p + 1)
                pool.tensor_tensor(row_int[:, slot, :, C_ID], row_int[:, 1 - slot, :, C_ID], step_ids[:, :], ALU.add
                                   ).then_inc(g_id, 1)
                pool.wait_ge(d_posf, p + 1)
                pool.sem_inc(g_gate)
                pool.tensor_copy(pos[:, slot], posf[:, :]).then_inc(g_pos, 1)
                pool.wait_ge(g_pos, p + 1)
                pool.wait_ge(g_id, p + 2)
                pool.wait_ge(d_w, p + 1)
                pool.sem_inc(g_gate)
                for g in range(G):
                    pool.indirect_dma_start(
                        out=scratch, out_offset=bass.IndirectOffsetOnAxis(ap=pos[:, slot, g:g + 1].bitcast(U32), axis=0),
                        in_=row[:, slot, g, :], in_offset=None, bounds_check=SCR - 1, oob_is_err=False,
                    ).then_inc(s_scat[slot], 16)

            def padding_rows(slot):
                pool.wait_ge(g_const, 2)
                experts = scratch.rearrange("(e n) c -> n e c", e=E)[0:P, slot * (E // 2):(slot + 1) * (E // 2)]
                pool.dma_start(experts, padt[:, :].rearrange("p (a c) -> p a c", a=1).to_broadcast([P, E // 2, ROW])
                               ).then_inc(s_scat[slot], 16)

            def tile(turn, k):
                pool.wait_ge(d_eo, turn * RING + k + 1)
                pool.sem_inc(g_gate)
                pool.indirect_dma_start(
                    out=out_rows, out_offset=bass.IndirectOffsetOnAxis(ap=eid[:, k:k + 1], axis=0),
                    in_=eo[:, k], in_offset=None, bounds_check=NTOK - 1, oob_is_err=False,
                ).then_inc(s_out[k], 16)

            def step(s, k, half):
                if live(s - 1):
                    powers(s - 1, 2, 1 - k)
                if live(s - 2):
                    scatter(s - 2, k, 16 + (half - 1) * 16 * G)
                if live(s + 2):
                    p = s + 2
                    wait(pool, d_h1T, p + 1)
                    wait(pool, pe_v, p)
                    pool.tensor_tensor(h1T_sum[:, :, :, :], h1T[0][:, :, :, :].bitcast(F32),
                                       h1T[1][:, :, :, :].bitcast(F32), ALU.add).then_inc(g_h1T, 1)
                if live(s + 1):
                    powers(s + 1, 1, 1 - k)
                if live(s + 2):
                    rotated(s + 2)
                if live(s + 3):
                    powers(s + 3, 0, 1 - k)
                if live(s + 1):
                    if isinstance(s, int) and s == -1:
                        pool.wait_ge(d_bvo, 1)
                    with_bias(s + 1, 1 - k)
                if isinstance(s, int) and s == NP:
                    for n in range(4):
                        tile(0, n)
                if isinstance(s, int) and s == -1:
                    padding_rows(0)
                    padding_rows(1)

            steps(pool, step)
            for n in range(4, RING):
                tile(0, n)
            with pool.Fori(1, TURNS) as i:
                for k in range(RING):
                    tile(i, k)


def constants():
    c = np.zeros((P, K_END), np.float32)
    c[:, K_ID:K_ID + P] = np.eye(P)
    half = D // 2
    inv = (1.0 / np.float32(10000.0) ** (np.arange(half, dtype=np.float32) / np.float32(half))).astype(np.float32)
    ang = (np.arange(T, dtype=np.float32)[None, :] * inv[:, None]).astype(np.float32)
    cos, sin = np.cos(ang).astype(np.float32), np.sin(ang).astype(np.float32)
    c[:, K_COS:K_COS + HALF * GT] = np.tile(cos, (1, HALF * G))
    c[:, K_SIN:K_SIN + GT] = np.tile(sin, (1, G))
    c[:, K_SIN + GT:K_SIN + 2 * GT] = np.tile(-sin, (1, G))
    t = np.arange(T)
    c[0:T, K_MASK:K_MASK + T] = np.where(t[None, :] <= t[:, None], 0.0, BIG)
    c[0:T, K_UP:K_UP + T] = t[:, None] < t[None, :]
    c[:, K_FALL:K_FALL + G * E] = np.tile(E - np.arange(E), G)
    c[:, K_EXP:K_EXP + E] = np.arange(E) * CAP + P
    turn = np.arange(TURNS)
    turn = np.where(turn < EARLY_TURNS, turn, turn - EARLY_TURNS)
    tile = (turn[:, None] * RING + np.minimum(np.arange(TW), RING - 1)).reshape(-1)
    c[:, K_TILE:K_TILE + TT] = tile
    c[:, K_TROW:K_TROW + TT] = tile * P
    c[:, K_FULL:K_FULL + E * FULL] = (np.arange(E)[:, None] * CAP + P + np.arange(FULL) * P).reshape(-1)
    return c


def by_halves(w):
    return np.ascontiguousarray(w.reshape(HALF, P, -1).transpose(1, 0, 2).reshape(P, -1))


def head_blocks(w):
    n = D // H
    full = np.zeros((HALF, n, H // HALF, n, H // HALF), w.dtype)
    for h in range(H):
        full[h % HALF, :, h // HALF, :, h // HALF] = w[:, :, h]
    return full.reshape(HALF, P, P).transpose(1, 0, 2).reshape(P, HALF * P)


def kernel(**inputs):
    import concourse.bacc as bacc
    from concourse.bass_utils import run_bass_kernel_spmd

    a = {n: np.asarray(v) for n, v in inputs.items()}
    ctx = a["ctx_1024"]
    nat = np.zeros((B, ST * P, D), ctx.dtype)
    nat[:, :S] = ctx
    nat = nat.reshape(B, ST, P, D).transpose(0, 2, 1, 3).reshape(B, P, NAT)
    trn = ctx.transpose(0, 2, 1).reshape(B, HALF, P, S).transpose(0, 2, 1, 3).reshape(B, P, TRN)
    both = np.concatenate([nat, trn], axis=2).reshape(NP, G, P, CW).transpose(0, 2, 1, 3).reshape(NP * P, G * CW)
    w_fold = np.concatenate([by_halves(a["L0_xattn_Wq"]), by_halves(a["L0_xattn_Wk"]), by_halves(a["L0_xattn_Wv"]),
                             by_halves(a["L0_xattn_Wo"].T)], axis=1)
    bv = np.repeat(a["L0_xattn_bv"].reshape(HALF, P).T, T, axis=1)
    b_fold = np.concatenate([a["L0_xattn_bq"].reshape(HALF, P).T, bv, np.tile(a["L0_xattn_bo"], (P, 1))], axis=1)
    w_router = np.concatenate([by_halves(a["L0_ffn_router_w"].T), np.tile(a["L0_ffn_router_b"], (P, G))], axis=1)
    w_expert = a["L0_ffn_expert_w"].transpose(0, 2, 1).reshape(E, HALF, P, D).transpose(2, 0, 1, 3).reshape(P, -1)
    arrays = {
        "x": a["x"], "ctxs": both, "consts": constants(),
        "w_self": np.concatenate([head_blocks(a[f"L0_attn_w_{n}"]) for n in "qkv"], axis=1),
        "w_fold": w_fold, "b_fold": b_fold, "w_router": w_router, "w_expert": w_expert,
        "b_expert": np.tile(a["L0_ffn_expert_b"].reshape(1, -1), (P, 1)),
    }
    arrays = {f"in_{n}": np.ascontiguousarray(v) for n, v in arrays.items()}
    nc = bacc.Bacc("TRN2", target_bir_lowering=False, num_devices=1)
    args = [nc.dram_tensor(n, v.shape, mybir.dt.from_np(v.dtype), kind="ExternalInput").ap()
            for n, v in arrays.items()]
    out = nc.dram_tensor("out", (B, T, D), F32, kind="ExternalOutput").ap()
    build(nc, *args, out)
    return run_bass_kernel_spmd(nc, [arrays], core_ids=[0]).results[0]["out"]
```
